# Optimizing a Trainium2 kernel written in Bass

```python
import numpy as np
import jax
import jax.numpy as jnp

def _softmax(x, axis=-1):
    return jax.nn.softmax(x, axis=axis)

def _gelu(x):
    return jax.nn.gelu(x, approximate=True)

def _silu(x):
    return jax.nn.silu(x)

def _sigmoid(x):
    return jax.nn.sigmoid(x)

def _layernorm(x, axis=-1, eps=1e-05):
    m = jnp.mean(x, axis=axis, keepdims=True)
    v = jnp.var(x, axis=axis, keepdims=True)
    return (x - m) / jnp.sqrt(v + eps)

def _scatter_add(tgt, idx, src, axis=0):
    return tgt.at[idx].add(src)

def _segment_sum(src, seg, n):
    return jax.ops.segment_sum(src, seg, n)
kernel_name = 'mk_dlrm_tower_d1_rec_r8_6e815f'

def setup_inputs(seed: int=0):
    np.random.seed(seed)
    _w = jnp.asarray

    def _rec_inputs():
        import jax
        import jax.numpy as jnp
        _tk = jax.random.key(seed)
        dense_ctx = jax.random.normal(jax.random.fold_in(_tk, 190), (512, 16), jnp.float32)
        ids = jnp.stack([jax.random.randint(jax.random.fold_in(_tk, 200 + f), (512,), 0, v, jnp.int32) for f, v in enumerate([125000, 125000, 1250, 1250, 1000, 125000, 125000, 1000, 125000, 12500, 12500, 125000, 125000, 1250, 1000, 1000, 1250, 1000, 12500, 1250, 1000, 1250, 12500, 12500, 12500, 12500])], axis=1)
        tbl_0 = 0.05 * jax.random.normal(jax.random.fold_in(_tk, 500 + 0), (125000, 32), jnp.float32)
        tbl_1 = 0.05 * jax.random.normal(jax.random.fold_in(_tk, 500 + 1), (125000, 32), jnp.float32)
        tbl_2 = 0.05 * jax.random.normal(jax.random.fold_in(_tk, 500 + 2), (1250, 32), jnp.float32)
        tbl_3 = 0.05 * jax.random.normal(jax.random.fold_in(_tk, 500 + 3), (1250, 32), jnp.float32)
        tbl_4 = 0.05 * jax.random.normal(jax.random.fold_in(_tk, 500 + 4), (1000, 32), jnp.float32)
        tbl_5 = 0.05 * jax.random.normal(jax.random.fold_in(_tk, 500 + 5), (125000, 32), jnp.float32)
        tbl_6 = 0.05 * jax.random.normal(jax.random.fold_in(_tk, 500 + 6), (125000, 32), jnp.float32)
        tbl_7 = 0.05 * jax.random.normal(jax.random.fold_in(_tk, 500 + 7), (1000, 32), jnp.float32)
        tbl_8 = 0.05 * jax.random.normal(jax.random.fold_in(_tk, 500 + 8), (125000, 32), jnp.float32)
        tbl_9 = 0.05 * jax.random.normal(jax.random.fold_in(_tk, 500 + 9), (12500, 32), jnp.float32)
        tbl_10 = 0.05 * jax.random.normal(jax.random.fold_in(_tk, 500 + 10), (12500, 32), jnp.float32)
        tbl_11 = 0.05 * jax.random.normal(jax.random.fold_in(_tk, 500 + 11), (125000, 32), jnp.float32)
        tbl_12 = 0.05 * jax.random.normal(jax.random.fold_in(_tk, 500 + 12), (125000, 32), jnp.float32)
        tbl_13 = 0.05 * jax.random.normal(jax.random.fold_in(_tk, 500 + 13), (1250, 32), jnp.float32)
        tbl_14 = 0.05 * jax.random.normal(jax.random.fold_in(_tk, 500 + 14), (1000, 32), jnp.float32)
        tbl_15 = 0.05 * jax.random.normal(jax.random.fold_in(_tk, 500 + 15), (1000, 32), jnp.float32)
        tbl_16 = 0.05 * jax.random.normal(jax.random.fold_in(_tk, 500 + 16), (1250, 32), jnp.float32)
        tbl_17 = 0.05 * jax.random.normal(jax.random.fold_in(_tk, 500 + 17), (1000, 32), jnp.float32)
        tbl_18 = 0.05 * jax.random.normal(jax.random.fold_in(_tk, 500 + 18), (12500, 32), jnp.float32)
        tbl_19 = 0.05 * jax.random.normal(jax.random.fold_in(_tk, 500 + 19), (1250, 32), jnp.float32)
        tbl_20 = 0.05 * jax.random.normal(jax.random.fold_in(_tk, 500 + 20), (1000, 32), jnp.float32)
        tbl_21 = 0.05 * jax.random.normal(jax.random.fold_in(_tk, 500 + 21), (1250, 32), jnp.float32)
        tbl_22 = 0.05 * jax.random.normal(jax.random.fold_in(_tk, 500 + 22), (12500, 32), jnp.float32)
        tbl_23 = 0.05 * jax.random.normal(jax.random.fold_in(_tk, 500 + 23), (12500, 32), jnp.float32)
        tbl_24 = 0.05 * jax.random.normal(jax.random.fold_in(_tk, 500 + 24), (12500, 32), jnp.float32)
        tbl_25 = 0.05 * jax.random.normal(jax.random.fold_in(_tk, 500 + 25), (12500, 32), jnp.float32)
        _rk = jax.random.fold_in(_tk, 7)
        W_top1 = 0.0606339 * jax.random.normal(jax.random.fold_in(_tk, 801), (272, 512), jnp.float32)
        W_top2 = 0.0441942 * jax.random.normal(jax.random.fold_in(_tk, 802), (512, 256), jnp.float32)
        W_top3 = 0.0625 * jax.random.normal(jax.random.fold_in(_tk, 803), (256, 1), jnp.float32)
        b_top1 = jnp.zeros((512,), jnp.float32)
        b_top2 = jnp.zeros((256,), jnp.float32)
        return (dense_ctx, ids, tbl_0, tbl_1, tbl_2, tbl_3, tbl_4, tbl_5, tbl_6, tbl_7, tbl_8, tbl_9, tbl_10, tbl_11, tbl_12, tbl_13, tbl_14, tbl_15, tbl_16, tbl_17, tbl_18, tbl_19, tbl_20, tbl_21, tbl_22, tbl_23, tbl_24, tbl_25, W_top1, b_top1, W_top2, b_top2, W_top3)
    dense_ctx, ids, tbl_0, tbl_1, tbl_2, tbl_3, tbl_4, tbl_5, tbl_6, tbl_7, tbl_8, tbl_9, tbl_10, tbl_11, tbl_12, tbl_13, tbl_14, tbl_15, tbl_16, tbl_17, tbl_18, tbl_19, tbl_20, tbl_21, tbl_22, tbl_23, tbl_24, tbl_25, W_top1, b_top1, W_top2, b_top2, W_top3 = _rec_inputs()

    def _L0_rec_setup():
        import jax, jax.numpy as jnp
        import numpy as np
        M_FIELDS = 26
        H1 = 128
        H2 = 128
        BATCH = 256
        EMB_K = 32

        def _cin_layer(x_prev, x0, W, b):
            return jnp.einsum('bik,bjk,hij->bhk', x_prev, x0, W) + b[None, :, None]
        key = jax.random.key(seed)
        k0, k1, k2, k3, k4 = jax.random.split(key, 5)
        inputs = jax.random.normal(k0, (BATCH, M_FIELDS, EMB_K), dtype=jnp.float32)
        W1 = jax.random.normal(k1, (H1, M_FIELDS, M_FIELDS), dtype=jnp.float32) * 0.05
        b1 = jax.random.normal(k2, (H1,), dtype=jnp.float32) * 0.05
        W2 = jax.random.normal(k3, (H2, H1, M_FIELDS), dtype=jnp.float32) * 0.05
        b2 = jax.random.normal(k4, (H2,), dtype=jnp.float32) * 0.05
        return {'inputs': inputs, 'W1': W1, 'b1': b1, 'W2': W2, 'b2': b2}
    _L0_rec_all = _L0_rec_setup()
    _L0_rec_in = {k: v for k, v in _L0_rec_all.items() if k in ('W1', 'b1', 'W2', 'b2')}
    del _L0_rec_all
    return {'dense_ctx': dense_ctx, 'ids': ids, 'tbl_0': tbl_0, 'tbl_1': tbl_1, 'tbl_2': tbl_2, 'tbl_3': tbl_3, 'tbl_4': tbl_4, 'tbl_5': tbl_5, 'tbl_6': tbl_6, 'tbl_7': tbl_7, 'tbl_8': tbl_8, 'tbl_9': tbl_9, 'tbl_10': tbl_10, 'tbl_11': tbl_11, 'tbl_12': tbl_12, 'tbl_13': tbl_13, 'tbl_14': tbl_14, 'tbl_15': tbl_15, 'tbl_16': tbl_16, 'tbl_17': tbl_17, 'tbl_18': tbl_18, 'tbl_19': tbl_19, 'tbl_20': tbl_20, 'tbl_21': tbl_21, 'tbl_22': tbl_22, 'tbl_23': tbl_23, 'tbl_24': tbl_24, 'tbl_25': tbl_25, 'W_top1': W_top1, 'b_top1': b_top1, 'W_top2': W_top2, 'b_top2': b_top2, 'W_top3': W_top3, 'L0_rec_W1': _L0_rec_in['W1'], 'L0_rec_b1': _L0_rec_in['b1'], 'L0_rec_W2': _L0_rec_in['W2'], 'L0_rec_b2': _L0_rec_in['b2']}

def reference(dense_ctx, ids, tbl_0, tbl_1, tbl_2, tbl_3, tbl_4, tbl_5, tbl_6, tbl_7, tbl_8, tbl_9, tbl_10, tbl_11, tbl_12, tbl_13, tbl_14, tbl_15, tbl_16, tbl_17, tbl_18, tbl_19, tbl_20, tbl_21, tbl_22, tbl_23, tbl_24, tbl_25, W_top1, b_top1, W_top2, b_top2, W_top3, L0_rec_W1, L0_rec_b1, L0_rec_W2, L0_rec_b2):
    import jax
    import jax.numpy as jnp

    def _L0_rec_ref(inputs, W1, b1, W2, b2):
        import jax, jax.numpy as jnp
        import numpy as np
        M_FIELDS = 26
        H1 = 128
        H2 = 128
        BATCH = 256
        EMB_K = 32

        def _cin_layer(x_prev, x0, W, b):
            return jnp.einsum('bik,bjk,hij->bhk', x_prev, x0, W) + b[None, :, None]
        x1 = _cin_layer(inputs, inputs, W1, b1)
        x2 = _cin_layer(x1, inputs, W2, b2)
        res = jnp.concatenate([x1, x2], axis=1)
        return jnp.sum(res, axis=-1)
    e = jnp.stack([tbl_0[ids[:, 0]], tbl_1[ids[:, 1]], tbl_2[ids[:, 2]], tbl_3[ids[:, 3]], tbl_4[ids[:, 4]], tbl_5[ids[:, 5]], tbl_6[ids[:, 6]], tbl_7[ids[:, 7]], tbl_8[ids[:, 8]], tbl_9[ids[:, 9]], tbl_10[ids[:, 10]], tbl_11[ids[:, 11]], tbl_12[ids[:, 12]], tbl_13[ids[:, 13]], tbl_14[ids[:, 14]], tbl_15[ids[:, 15]], tbl_16[ids[:, 16]], tbl_17[ids[:, 17]], tbl_18[ids[:, 18]], tbl_19[ids[:, 19]], tbl_20[ids[:, 20]], tbl_21[ids[:, 21]], tbl_22[ids[:, 22]], tbl_23[ids[:, 23]], tbl_24[ids[:, 24]], tbl_25[ids[:, 25]]], axis=1)
    z = _L0_rec_ref(e, L0_rec_W1, L0_rec_b1, L0_rec_W2, L0_rec_b2)
    z = z.reshape(z.shape[0], -1)
    h = jnp.concatenate([z, dense_ctx], axis=1)
    h = jnp.maximum(h @ W_top1 + b_top1, 0.0)
    h = jnp.maximum(h @ W_top2 + b_top2, 0.0)
    y = h @ W_top3
    return y

_drawn_inputs = setup_inputs


def setup_inputs(seed=0):
    import zlib

    import numpy as np

    out = dict(_drawn_inputs(seed))
    spreads = {'b_top1': (0.0, 2.0), 'b_top2': (0.0, 0.8)}
    factors = {'tbl_0': 8.0,
     'tbl_1': 8.0,
     'tbl_2': 8.0,
     'tbl_3': 8.0,
     'tbl_4': 8.0,
     'tbl_5': 8.0,
     'tbl_6': 8.0,
     'tbl_7': 8.0,
     'tbl_8': 8.0,
     'tbl_9': 8.0,
     'tbl_10': 8.0,
     'tbl_11': 8.0,
     'tbl_12': 8.0,
     'tbl_13': 8.0,
     'tbl_14': 8.0,
     'tbl_15': 8.0,
     'tbl_16': 8.0,
     'tbl_17': 8.0,
     'tbl_18': 8.0,
     'tbl_19': 8.0,
     'tbl_20': 8.0,
     'tbl_21': 8.0,
     'tbl_22': 8.0,
     'tbl_23': 8.0,
     'tbl_24': 8.0,
     'tbl_25': 8.0,
     'L0_rec_W1': 8.0,
     'L0_rec_W2': 4.141,
     'dense_ctx': 5.906}
    for name, (base, spread) in spreads.items():
        noise = np.random.default_rng([zlib.crc32(name.encode()), seed]).standard_normal(out[name].shape)
        drawn = base * np.exp(spread * noise) if base else spread * noise
        out[name] = jnp.asarray(drawn.astype(out[name].dtype))
    for name, factor in factors.items():
        out[name] = (out[name] * factor).astype(out[name].dtype)
    return out
```

```python
from contextlib import ExitStack

import concourse.bass as bass
from concourse import mybir

F32 = mybir.dt.float32
I32 = mybir.dt.int32
U32 = mybir.dt.uint32
ALU = mybir.AluOpType
ACT = mybir.ActivationFunctionType

P = 128
SQ = 32
B, F, K, H = 512, 26, 32, 128
NQ = B // P
NG = P // SQ
ND, N1, N2 = 16, 512, 256
M1, M2 = N1 // P, N2 // P

CLIQUES = [(0, 7), (7, 6), (13, 1), (14, 12)]
START = [0]
for _, n in CLIQUES:
    START.append(START[-1] + n * (n + 1) // 2)
LIST1 = START[-1]
C0, C1, C2, C3 = (n for _, n in CLIQUES)
L2 = C0 + C1
NL2 = F - L2
A0 = L2 + C2
XB = LIST1
SB = XB + A0 * C3
RB = SB + C0 * (C1 + C2)
UB = RB + C1 * C2
NCOL = UB + 1
LIST2 = UB - SB
EF = 64
NS = EF + F
NP = P + NS
assert LIST1 == P and LIST2 <= EF and UB == F * (F + 1) // 2

NS1 = (F + 1) * NG
NS2 = (NL2 + 1) * NG
HALF = SQ // 2
G1, G2 = 4, 8
CB = 3


def build(nc, ids, tables, dense_t, w1, w2_t, columns, w_top1, w_top2, y):
    with ExitStack() as ctx:
        def sb(name, shape, dt=F32):
            return ctx.enter_context(nc.sbuf_tensor(name, shape, dt))

        def sem(name):
            return ctx.enter_context(nc.semaphore(name))

        idx = sb("idx", [P, NQ, F], I32)
        emb = sb("emb", [P, 2, F * K])
        emb_t = sb("emb_t", [P, 2, F, SQ])
        prod = sb("prod", [P, SQ, NP])
        diag = sb("diag", [P, SQ, F + 1, NG])
        sums1 = sb("sums1", [P, 2, F + 1, P])
        sums2 = sb("sums2", [NS, 2, NL2 + 1, P])
        cross = sb("cross", [P, CB, P])
        ident = sb("ident", [P, P])
        w1_sb = sb("w1_sb", [P, F, F])
        w2_sb = sb("w2_sb", [P, F, P])
        w1_pairs = sb("w1_pairs", [P, NCOL])
        w1_cross = sb("w1_cross", [P, CB, P])
        vmat = sb("vmat", [P, F, NCOL])
        u_pad = sb("u_pad", [P, NS])
        v1_t = sb("v1_t", [P, F, P])
        v2_t = sb("v2_t", [EF, NL2, P])
        z1w = sb("z1w", [P, 2 + CB, P])
        z2u = sb("z2u", [NS, P])
        cols_sb = sb("cols_sb", [P, 2 + M1 + 2 * M2])
        b12 = cols_sb[:, 0:2]
        bt1 = cols_sb[:, 2:2 + M1]
        bt2 = cols_sb[:, 2 + M1:2 + M1 + M2]
        wt3 = cols_sb[:, 2 + M1 + M2:]
        kbias = sb("kbias", [P, 2])
        wt1 = sb("wt1", [P, 2, N1])
        wt1_d = sb("wt1_d", [ND, N1])
        wt2 = sb("wt2", [P, M1, N2])
        dense = sb("dense", [ND, NQ, P])
        z_sb = sb("z_sb", [P, 2, P])
        h1_sb = sb("h1_sb", [P, M1, P])
        h2_sb = sb("h2_sb", [P, M2, P])
        y_sb = sb("y_sb", [1, B])

        bank = [ctx.enter_context(nc.psum_tensor(f"bank{i}", [P, 512], F32)) for i in range(8)]
        sum1_banks, sum2_banks = bank[0:4], bank[4:6]
        z_bank, mlp_bank = bank[6], bank[7]

        ids_in = sem("ids_in")
        cin_in = sem("cin_in")
        w2_in = sem("w2_in")
        mlp_in = sem("mlp_in")
        gathered = [sem(f"gathered{q}") for q in range(NQ)]
        ident_cleared = sem("ident_cleared")
        ident_made = sem("ident_made")
        cleared = sem("cleared")
        halved = sem("halved")
        pairs_built = sem("pairs_built")
        cross_built = sem("cross_built")
        v_filled = sem("v_filled")
        v_out_act = sem("v_out_act")
        v_out_dve = sem("v_out_dve")
        v_folded = sem("v_folded")
        turned_filled = sem("turned_filled")
        turned_out = sem("turned_out")
        emb_turned = sem("emb_turned")
        prod_ready = sem("prod_ready")
        diag_ready = sem("diag_ready")
        sum1_filled = sem("sum1_filled")
        sum1_out = sem("sum1_out")
        sum2_filled = sem("sum2_filled")
        sum2_out = sem("sum2_out")
        cross_ready = sem("cross_ready")
        z_filled = sem("z_filled")
        z_ready = sem("z_ready")
        h1_filled = sem("h1_filled")
        h1_ready = sem("h1_ready")
        h2_filled = sem("h2_filled")
        h2_ready = sem("h2_ready")
        y_filled = sem("y_filled")
        y_ready = sem("y_ready")
        stored = sem("stored")

        block = ctx.enter_context(nc.Block())

        turns = [(w1_pairs[:, 0:LIST1], z1w[:, 0, :]), (w1_pairs[:, SB:UB], z1w[0:LIST2, 1, :])]
        turns += [(w1_cross[:, s, :], z1w[:, 2 + s, :]) for s in range(CB)]
        turns += [(u_pad[:, :], z2u[:, :])]
        W1_TURNS = len(turns)
        turns += [(vmat[:, l, 0:LIST1], v1_t[:, l, :]) for l in range(F)]
        turns += [(vmat[:, L2 + l, SB:UB], v2_t[0:LIST2, l, :]) for l in range(NL2)]

        def half_used(q, half):
            return q * (SQ // G2) + (half + 1) * (HALF // G2)

        @block.sync
        def _(sp):
            sp.dma_start(idx[:], ids.rearrange("(q p) f -> p q f", p=P)).then_inc(ids_in, 16)
            sp.dma_start(w1_sb[:], w1).then_inc(cin_in, 16)
            sp.dma_start(cols_sb[:], columns).then_inc(cin_in, 16)
            sp.dma_start(w2_sb[:], w2_t).then_inc(w2_in, 16)
            sp.dma_start(wt1[:], w_top1[0:2 * P].rearrange("(c p) n -> p c n", p=P)).then_inc(mlp_in, 16)
            sp.dma_start(wt1_d[:], w_top1[2 * P:]).then_inc(mlp_in, 16)
            sp.dma_start(wt2[:], w_top2.rearrange("(c p) n -> p c n", p=P)).then_inc(mlp_in, 16)
            sp.dma_start(dense[:], dense_t).then_inc(mlp_in, 16)
            sp.wait_ge(y_ready, NQ)
            sp.dma_start(y.rearrange("b o -> o b"), y_sb[:]).then_inc(stored, 16)
            sp.wait_ge(stored, 16)

        @block.gpsimd
        def _(pool):
            nc.gpsimd.memset(ident[:], 0.0).then_inc(ident_cleared, 1)
            pool.wait_ge(ident_cleared, 1)
            nc.gpsimd.affine_select(out=ident[:], in_=ident[:], compare_op=ALU.not_equal, fill=1.0, base=0,
                                    pattern=[[-1, P]], channel_multiplier=1).then_inc(ident_made, 1)
            pool.wait_ge(ids_in, 16)
            for q in range(NQ):
                if q >= 2:
                    pool.wait_ge(emb_turned, q - 1)
                for f in range(F):
                    nc.gpsimd.indirect_dma_start(
                        out=emb[:, q % 2, f * K:(f + 1) * K], out_offset=None, in_=tables[f],
                        in_offset=bass.IndirectOffsetOnAxis(ap=idx[:, q, f:f + 1].bitcast(U32), axis=0),
                    ).then_inc(gathered[q], 16)

        @block.tensor
        def _(pe):
            pe.wait_ge(pairs_built, 1)
            pe.wait_ge(w2_in, 16)
            for l in range(F):
                if l >= 4:
                    pe.wait_ge(v_out_act if l % 2 == 0 else v_out_dve, (l - 4) // 2 + 1)
                nc.tensor.matmul(bank[l % 4][:, 0:NCOL], w2_sb[:, l, :], w1_pairs[:, :],
                                 start=True, stop=True).then_inc(v_filled, 1)

            pe.wait_ge(ident_made, 1)
            pe.wait_ge(cross_built, 1)
            pe.wait_ge(v_folded, 1)
            for n, (src, _) in enumerate(turns):
                if n == W1_TURNS:
                    pe.wait_ge(v_folded, 3)
                if n % 4 == 0 and n >= 16:
                    pe.wait_ge(turned_out, n // 4 - 3)
                rows = src.shape[1]
                mm = nc.tensor.transpose(bank[n // 4 % 4][0:rows, n % 4 * P:(n % 4 + 1) * P], src, ident[:])
                if n % 4 == 3 or n == len(turns) - 1:
                    mm.then_inc(turned_filled, 1)
            pe.wait_ge(turned_out, (len(turns) + 3) // 4)

            for q in range(NQ):
                for t in range(SQ):
                    if t % HALF == 0:
                        pe.wait_ge(prod_ready, 2 * q + t // HALF + 1)
                        pe.wait_ge(diag_ready, 2 * q + t // HALF + 1)
                    n1, n2 = q * (SQ // G1) + t // G1, q * (SQ // G2) + t // G2
                    if t % G1 == 0 and n1 >= 4:
                        pe.wait_ge(sum1_out, n1 - 3)
                    if t % G2 == 0 and n2 >= 2:
                        pe.wait_ge(sum2_out, n2 - 1)
                    moving = diag[:, t].rearrange("p l g -> p (l g)")
                    o1, o2 = t % G1 * NS1, t % G2 * NS2
                    mm = nc.tensor.matmul(sum1_banks[n1 % 4][:, o1:o1 + NS1], prod[:, t, 0:P], moving,
                                          start=True, stop=True)
                    if t % G1 == G1 - 1:
                        mm.then_inc(sum1_filled, 1)
                    mm = nc.tensor.matmul(sum2_banks[n2 % 2][0:NS, o2:o2 + NS2], prod[:, t, P:NP],
                                          moving[:, NG * L2:], start=True, stop=True)
                    if t % G2 == G2 - 1:
                        mm.then_inc(sum2_filled, 1)
                pe.wait_ge(sum1_out, (q + 1) * (SQ // G1))
                pe.wait_ge(sum2_out, (q + 1) * (SQ // G2))

                s = q % 2
                z2, z1 = z_bank[:, 0:P], z_bank[:, P:2 * P]
                for l in range(F):
                    nc.tensor.matmul(z2, v1_t[:, l, :], sums1[:, s, l, :], start=(l == 0), stop=False)
                for l in range(NL2):
                    nc.tensor.matmul(z2, v2_t[0:LIST2, l, :], sums2[0:LIST2, s, l, :], start=False, stop=False)
                nc.tensor.matmul(z2, z2u[:, :], sums2[:, s, NL2, :], start=False, stop=True)
                nc.tensor.matmul(z1, z1w[:, 0, :], sums1[:, s, F, :], start=True, stop=False)
                nc.tensor.matmul(z1, z1w[0:LIST2, 1, :], sums2[0:LIST2, s, NL2, :], start=False, stop=False)
                pe.wait_ge(cross_ready, q + 1)
                for c in range(CB):
                    mm = nc.tensor.matmul(z1, z1w[:, 2 + c, :], cross[:, c, :], start=False, stop=(c == CB - 1))
                mm.then_inc(z_filled, 1)

                if q == 0:
                    pe.wait_ge(mlp_in, 16 * 4)
                pe.wait_ge(z_ready, q + 1)
                if q:
                    pe.wait_ge(y_ready, q)
                for m in range(M1):
                    cols = slice(m * P, (m + 1) * P)
                    nc.tensor.matmul(mlp_bank[:, cols], wt1[:, 0, cols], z_sb[:, 0, :], start=True, stop=False)
                    nc.tensor.matmul(mlp_bank[:, cols], wt1[:, 1, cols], z_sb[:, 1, :], start=False, stop=False)
                    mm = nc.tensor.matmul(mlp_bank[:, cols], wt1_d[:, cols], dense[:, q, :], start=False, stop=True)
                mm.then_inc(h1_filled, 1)
                pe.wait_ge(h1_ready, q + 1)
                for m in range(M2):
                    for c in range(M1):
                        mm = nc.tensor.matmul(z_bank[:, (2 + m) * P:(3 + m) * P], wt2[:, c, m * P:(m + 1) * P],
                                              h1_sb[:, c, :], start=(c == 0), stop=(c == M1 - 1))
                mm.then_inc(h2_filled, 1)
                pe.wait_ge(h2_ready, q + 1)
                for c in range(M2):
                    mm = nc.tensor.matmul(mlp_bank[0:1, 0:P], wt3[:, c:c + 1], h2_sb[:, c, :],
                                          start=(c == 0), stop=(c == M2 - 1))
                mm.then_inc(y_filled, 1)

        @block.scalar
        def _(act):
            for l in range(0, F, 2):
                act.wait_ge(v_filled, l + 1)
                nc.scalar.activation(vmat[:, l, :], bank[l % 4][:, 0:NCOL], ACT.Copy).then_inc(v_out_act, 1)
            for n in range((len(turns) + 3) // 4):
                act.wait_ge(turned_filled, n + 1)
                for i, (src, dst) in enumerate(turns[4 * n:4 * n + 4]):
                    last = nc.scalar.activation(dst, bank[n % 4][0:src.shape[1], i * P:(i + 1) * P], ACT.Copy)
                last.then_inc(turned_out, 1)

            for q in range(NQ):
                act.wait_ge(emb_turned, q + 1)
                if q == 0:
                    act.wait_ge(cleared, 1)
                for half in range(2):
                    if q:
                        act.wait_ge(sum2_filled, half_used(q - 1, half))
                    ts = slice(half * HALF, (half + 1) * HALF)
                    for g in range(NG):
                        rows = slice(g * SQ, (g + 1) * SQ)
                        last = nc.scalar.activation(
                            diag[rows, ts, 0:F, g], emb_t[rows, q % 2, :, ts].rearrange("p f t -> p t f"), ACT.Copy)
                    last.then_inc(diag_ready, 1)
                for n in range(SQ // G1):
                    act.wait_ge(sum1_filled, q * (SQ // G1) + n + 1)
                    if q >= 2 and n == 0:
                        act.wait_ge(z_filled, q - 1)
                    src = sum1_banks[n % 4][:, 0:G1 * NS1].rearrange("p (t l g) -> p l t g", t=G1, g=NG)
                    dst = sums1[:, q % 2, :, n * G1 * NG:(n + 1) * G1 * NG].rearrange("p l (t g) -> p l t g", g=NG)
                    nc.scalar.activation(dst, src, ACT.Copy).then_inc(sum1_out, 1)
                    if n % 2:
                        m = n // 2
                        act.wait_ge(sum2_filled, q * (SQ // G2) + m + 1)
                        src = sum2_banks[m % 2][0:NS, 0:G2 * NS2].rearrange("p (t l g) -> p l t g", t=G2, g=NG)
                        dst = sums2[:, q % 2, :, m * G2 * NG:(m + 1) * G2 * NG].rearrange("p l (t g) -> p l t g", g=NG)
                        nc.scalar.activation(dst, src, ACT.Copy).then_inc(sum2_out, 1)

                act.wait_ge(z_filled, q + 1)
                if q == 0:
                    act.wait_ge(cin_in, 32)
                    act.wait_ge(cross_built, 1)
                nc.scalar.activation(z_sb[:, 0, :], z_bank[:, P:2 * P], ACT.Identity, bias=kbias[:, 0:1])
                nc.scalar.activation(z_sb[:, 1, :], z_bank[:, 0:P], ACT.Identity,
                                     bias=kbias[:, 1:2]).then_inc(z_ready, 1)
                if q == 0:
                    act.wait_ge(mlp_in, 16 * 4)
                act.wait_ge(h1_filled, q + 1)
                for m in range(M1):
                    last = nc.scalar.activation(h1_sb[:, m, :], mlp_bank[:, m * P:(m + 1) * P], ACT.Relu,
                                                bias=bt1[:, m:m + 1])
                last.then_inc(h1_ready, 1)
                act.wait_ge(h2_filled, q + 1)
                for m in range(M2):
                    last = nc.scalar.activation(h2_sb[:, m, :], z_bank[:, (2 + m) * P:(3 + m) * P], ACT.Relu,
                                                bias=bt2[:, m:m + 1])
                last.then_inc(h2_ready, 1)
                act.wait_ge(y_filled, q + 1)
                nc.scalar.activation(y_sb[:, q * P:(q + 1) * P].rearrange("o (g t) -> o t g", g=NG),
                                     mlp_bank[0:1, 0:P].rearrange("o (t g) -> o t g", g=NG),
                                     ACT.Copy).then_inc(y_ready, 1)

        @block.vector
        def _(dve):
            nc.vector.memset(diag[:], 0.0)
            nc.vector.memset(prod[:, :, P + LIST2:P + EF], 0.0)
            nc.vector.memset(cross[:], 0.0)
            nc.vector.memset(w1_cross[:], 0.0)
            nc.vector.memset(u_pad[:], 0.0).then_inc(cleared, 1)
            dve.wait_ge(cleared, 1)
            for g in range(NG):
                last = nc.vector.memset(diag[g * SQ:(g + 1) * SQ, :, F, g], 1.0)
            last.then_inc(cleared, 1)

            dve.wait_ge(cin_in, 32)
            eye = w1_sb[:].rearrange("p a b -> p (a b)")[:, 0:F * F:F + 1]
            nc.vector.tensor_scalar(eye, eye, 0.5, None, ALU.mult).then_inc(halved, 1)
            dve.wait_ge(halved, 1)
            for c, (f0, n) in enumerate(CLIQUES):
                for j in range(n):
                    o = START[c] + j * (j + 1) // 2
                    nc.vector.tensor_tensor(w1_pairs[:, o:o + j + 1], w1_sb[:, f0:f0 + j + 1, f0 + j],
                                            w1_sb[:, f0 + j, f0:f0 + j + 1], ALU.add)
            for o, u0, nu, v0, nv in ((XB, 0, A0, A0, C3), (SB, 0, C0, C0, C1 + C2), (RB, C0, C1, L2, C2)):
                nc.vector.tensor_tensor(
                    w1_pairs[:, o:o + nu * nv].rearrange("p (u v) -> p u v", v=nv),
                    w1_sb[:, u0:u0 + nu, v0:v0 + nv],
                    w1_sb[:, v0:v0 + nv, u0:u0 + nu].rearrange("p v u -> p u v"), ALU.add)
            nc.vector.tensor_copy(w1_pairs[:, UB:NCOL], cols_sb[:, 0:1]).then_inc(pairs_built, 1)
            nc.vector.tensor_scalar(kbias[:], b12, float(K), None, ALU.mult)
            dve.wait_ge(pairs_built, 1)
            for a in range(C3):
                last = nc.vector.tensor_copy(w1_cross[:, a % CB, a // CB * SQ:a // CB * SQ + A0],
                                             w1_pairs[:, XB + a:SB:C3])
            last.then_inc(cross_built, 1)

            for l in range(1, F, 2):
                dve.wait_ge(v_filled, l + 1)
                nc.vector.tensor_copy(vmat[:, l, :], bank[l % 4][:, 0:NCOL]).then_inc(v_out_dve, 1)

            dve.wait_ge(v_out_act, F // 2)
            dve.wait_ge(v_out_dve, F // 2)
            x = vmat[:, :, XB:SB].rearrange("p l (u a) -> p l u a", a=C3)
            s_ = vmat[:, :, SB:RB].rearrange("p l (u v) -> p l u v", v=C1 + C2)
            r = vmat[:, :, RB:UB]
            nc.vector.tensor_copy(u_pad[:, EF:NS], vmat[:, :, UB]).then_inc(v_folded, 1)

            def add(dst, term):
                return nc.vector.tensor_tensor(dst, dst, term, ALU.add)

            for second in range(2):
                for c, (f0, n) in enumerate(CLIQUES):
                    for j in range(n):
                        m = j if second else j + 1
                        if m == 0:
                            continue
                        o = START[c] + j * (j + 1) // 2

                        def term(pairs):
                            if second:
                                return pairs[:, f0:f0 + m, j, :].rearrange("p i v -> p v i")
                            return pairs[:, f0 + j, 0:m, :].rearrange("p i v -> p v i")
                        if c == 3:
                            t3 = x[:, f0:f0 + m, :, j].rearrange("p i u -> p u i") if second else x[:, f0 + j, :, 0:m]
                            add(vmat[:, 0:A0, o:o + m], t3)
                        else:
                            add(vmat[:, A0:F, o:o + m], term(x[:, :, f0:f0 + n]))
                        if c == 0:
                            add(vmat[:, C0:A0, o:o + m], term(s_))
                        if c == 1:
                            t1 = s_[:, f0:f0 + m, :, j].rearrange("p i u -> p u i") if second else s_[:, f0 + j, :, 0:m]
                            add(vmat[:, 0:C0, o:o + m], t1)
                            t2 = r[:, f0:f0 + m, j] if second else r[:, f0 + j, 0:m]
                            add(vmat[:, L2, o:o + m], t2)
                for v in range(C1 + C2):
                    dst = vmat[:, A0:F, SB + v:RB:C1 + C2]
                    if second:
                        add(dst, x[:, 0:C0, C0 + v, :].rearrange("p u a -> p a u"))
                    else:
                        add(dst, x[:, C0 + v, 0:C0, :].rearrange("p u a -> p a u"))
                dst = vmat[:, A0:F, RB:UB]
                last = add(dst, x[:, C0:L2, L2, :].rearrange("p v a -> p a v") if second
                           else x[:, L2, C0:L2, :].rearrange("p v a -> p a v"))
                dst = s_[:, L2, :, 0:C1]
                last = add(dst, r[:, 0:C0, :] if second
                           else s_[:, C0:L2, :, C1].rearrange("p v u -> p u v"))
                last.then_inc(v_folded, 1)
                if not second:
                    dve.wait_ge(v_folded, 2)

            for q in range(NQ):
                dve.wait_ge(gathered[q], 16 * F)
                if q >= 2:
                    dve.wait_ge(diag_ready, 2 * q - 2)
                et = emb_t[:, q % 2]
                nc.vector.transpose(et.rearrange("p f t -> p (f t)"), emb[:, q % 2]).then_inc(emb_turned, 1)
                dve.wait_ge(emb_turned, q + 1)
                for half in range(2):
                    if q:
                        dve.wait_ge(sum2_filled, half_used(q - 1, half))
                    ts = slice(half * HALF, (half + 1) * HALF)

                    def fields(a, n):
                        return et[:, a:a + n, ts].rearrange("p f t -> p t f")

                    for c, (f0, n) in enumerate(CLIQUES):
                        for j in range(n):
                            o = START[c] + j * (j + 1) // 2
                            nc.vector.tensor_tensor(prod[:, ts, o:o + j + 1], fields(f0, j + 1),
                                                    fields(f0 + j, 1).to_broadcast([P, HALF, j + 1]), ALU.mult)
                    o = P
                    for v in range(C0):
                        nv = C1 + C2
                        nc.vector.tensor_tensor(prod[:, ts, o:o + nv], fields(C0, nv),
                                                fields(v, 1).to_broadcast([P, HALF, nv]), ALU.mult)
                        o += nv
                    nc.vector.tensor_tensor(prod[:, ts, o:o + C1], fields(C0, C1),
                                            fields(L2, 1).to_broadcast([P, HALF, C1]), ALU.mult)
                    nc.vector.tensor_copy(prod[:, ts, P + EF:NP], fields(0, F)).then_inc(prod_ready, 1)

                dve.wait_ge(sum2_out, (q + 1) * (SQ // G2))
                if q:
                    dve.wait_ge(z_filled, q)
                for g in range(NG):
                    a = A0 - L2 + CB * g
                    last = nc.vector.tensor_copy(cross[g * SQ:g * SQ + A0, :, :],
                                                 sums2[EF:EF + A0, q % 2, a:a + CB, :])
                last.then_inc(cross_ready, 1)


def kernel(**inputs):
    import numpy as np
    import concourse.bacc as bacc
    from concourse.bass_utils import run_bass_kernel_spmd as run

    nc = bacc.Bacc("TRN2", target_bir_lowering=False, num_devices=1)
    arrays = {}

    def give(name, a):
        a = np.ascontiguousarray(a)
        arrays["in_" + name] = a
        return nc.dram_tensor("in_" + name, a.shape, mybir.dt.from_np(a.dtype), kind="ExternalInput").ap()

    ids = give("ids", inputs["ids"])
    tables = [give(f"tbl_{f}", inputs[f"tbl_{f}"]) for f in range(F)]
    dense_t = give("dense_t", np.asarray(inputs["dense_ctx"]).reshape(NQ, NG, SQ, ND).transpose(3, 0, 2, 1)
                   .reshape(ND, NQ, P))
    w1 = give("w1", inputs["L0_rec_W1"])
    w2_t = give("w2_t", np.asarray(inputs["L0_rec_W2"]).transpose(1, 2, 0))
    vectors = [np.asarray(inputs[n]).reshape(-1, P) for n in ("L0_rec_b1", "L0_rec_b2", "b_top1", "b_top2", "W_top3")]
    columns = give("columns", np.concatenate(vectors).T)
    y = nc.dram_tensor("out_y", (B, 1), F32, kind="ExternalOutput").ap()
    build(nc, ids, tables, dense_t, w1, w2_t, columns, give("W_top1", inputs["W_top1"]),
          give("W_top2", inputs["W_top2"]), y)
    r = run(nc, [arrays], core_ids=[0])
    return r.results[0]["out_y"]
```

```python
from contextlib import ExitStack

import concourse.bass as bass
from concourse import mybir

F32 = mybir.dt.float32
I32 = mybir.dt.int32
U32 = mybir.dt.uint32
ALU = mybir.AluOpType
ACT = mybir.ActivationFunctionType

P = 128
SQ = 32
B, F, K, H = 512, 26, 32, 128
NQ = B // P
NG = P // SQ
ND, N1, N2 = 16, 512, 256
M1, M2 = N1 // P, N2 // P

CLIQUES = [(0, 7), (7, 6), (13, 1), (14, 12)]
START = [0]
for _, n in CLIQUES:
    START.append(START[-1] + n * (n + 1) // 2)
LIST1 = START[-1]
C0, C1, C2, C3 = (n for _, n in CLIQUES)
L2 = C0 + C1
NL2 = F - L2
A0 = L2 + C2
XB = LIST1
GAP = XB + A0 * C3
SB = GAP + F
RB = SB + C0 * (C1 + C2)
UB = RB + C1 * C2
NCOL = UB + 1
LIST2 = UB - SB
NS = F + LIST2
NP = P + NS
assert LIST1 == P and LIST1 + A0 * C3 + LIST2 == F * (F + 1) // 2

NS1 = (F + 1) * NG
NS2 = (NL2 + 1) * NG
PARTS = ((0, A0), (A0, C3))
HALF = SQ // 2
G1, G2 = 4, 8
CB = 3


def build(nc, ids, tables, dense_t, w1, w2_t, columns, w_top1, w_top2, y):
    with ExitStack() as ctx:
        def sb(name, shape, dt=F32):
            return ctx.enter_context(nc.sbuf_tensor(name, shape, dt))

        def sem(name):
            return ctx.enter_context(nc.semaphore(name))

        idx = sb("idx", [P, NQ, F], I32)
        emb = sb("emb", [P, 2, F * K])
        emb_t = sb("emb_t", [P, 2, F, SQ])
        prod = sb("prod", [P, SQ, NP])
        w2_sb = prod[:].rearrange("p t n -> p (t n)")[:, 0:F * P].rearrange("p (l h) -> p l h", h=P)
        diag = sb("diag", [P, SQ, F + 1, NG])
        sums1 = sb("sums1", [P, F + 1, P])
        sums2 = sb("sums2", [NS, NL2 + 1, P])
        cross = sb("cross", [P, CB, P])
        ident = sb("ident", [P, P])
        w1_sb = sb("w1_sb", [P, F, F])
        w1_pairs = sb("w1_pairs", [P, NCOL])
        w1_cross = sb("w1_cross", [P, CB, P])
        vmat = sb("vmat", [P, F, NCOL])
        u_pad = sb("u_pad", [P, NS])
        wgt1 = sb("wgt1", [P, 1 + CB + F, P])
        wgt2 = sb("wgt2", [NS, 2 + NL2, P])
        cols_sb = sb("cols_sb", [P, 2 + M1 + 2 * M2])
        b12 = cols_sb[:, 0:2]
        bt1 = cols_sb[:, 2:2 + M1]
        bt2 = cols_sb[:, 2 + M1:2 + M1 + M2]
        wt3 = cols_sb[:, 2 + M1 + M2:]
        kbias = sb("kbias", [P, 2])
        wt1 = sb("wt1", [P, 2, N1])
        wt1_d = sb("wt1_d", [ND, N1])
        wt2 = sb("wt2", [P, M1, N2])
        dense = sb("dense", [ND, NQ, P])
        z_sb = sb("z_sb", [P, 2, P])
        h1_sb = sb("h1_sb", [P, M1, P])
        h2_sb = sb("h2_sb", [P, M2, P])
        y_sb = sb("y_sb", [1, B])

        bank = [ctx.enter_context(nc.psum_tensor(f"bank{i}", [P, 512], F32)) for i in range(8)]
        sum1_banks, sum2_banks = bank[0:4], bank[4:6]
        z_bank, mlp_bank = bank[6], bank[7]

        ids_in = sem("ids_in")
        cin_in = sem("cin_in")
        w2_in = sem("w2_in")
        mlp_in = sem("mlp_in")
        gathered = [[sem(f"gathered{q}_{part}") for part in ("low", "high")] for q in range(NQ)]
        ident_cleared = sem("ident_cleared")
        ident_made = sem("ident_made")
        cleared = sem("cleared")
        halved = sem("halved")
        pairs_built = sem("pairs_built")
        cross_built = sem("cross_built")
        v_filled = sem("v_filled")
        v_out_act = sem("v_out_act")
        v_out_dve = sem("v_out_dve")
        v_folded = sem("v_folded")
        turned_filled = sem("turned_filled")
        turned_out = sem("turned_out")
        emb_turned = sem("emb_turned")
        prod_ready = sem("prod_ready")
        diag_ready = sem("diag_ready")
        sum1_filled = sem("sum1_filled")
        sum1_out = sem("sum1_out")
        sum2_filled = sem("sum2_filled")
        sum2_out = sem("sum2_out")
        cross_ready = sem("cross_ready")
        z_filled = sem("z_filled")
        z_ready = sem("z_ready")
        h1_filled = sem("h1_filled")
        h1_ready = sem("h1_ready")
        h2_filled = sem("h2_filled")
        h2_ready = sem("h2_ready")
        y_filled = sem("y_filled")
        y_ready = sem("y_ready")
        stored = sem("stored")

        block = ctx.enter_context(nc.Block())

        one = [w1_pairs[:, 0:LIST1]] + [w1_cross[:, c, :] for c in range(CB)] + [vmat[:, l, 0:LIST1] for l in range(F)]
        two = [w1_pairs[:, GAP:UB], u_pad[:, :]] + [vmat[:, L2 + l, GAP:UB] for l in range(NL2)]
        turns = [(sources[i:i + 4], wgt, i) for sources, wgt in ((one, wgt1), (two, wgt2))
                 for i in range(0, len(sources), 4)]
        T1, T2 = SQ // G1, SQ // G2

        def half_used(q, half):
            return q * (SQ // G2) + (half + 1) * (HALF // G2)

        def in_psum(src, steps, width):
            return src[:, 0:steps * width].rearrange("p (t l g) -> p l t g", t=steps, g=NG)

        def in_sbuf(dst, n, steps):
            return dst[:, :, n * steps * NG:(n + 1) * steps * NG].rearrange("p l (t g) -> p l t g", g=NG)

        @block.sync
        def _(sp):
            sp.dma_start(idx[:], ids.rearrange("(q p) f -> p q f", p=P)).then_inc(ids_in, 16)
            sp.dma_start(w1_sb[:], w1).then_inc(cin_in, 16)
            sp.dma_start(cols_sb[:], columns).then_inc(cin_in, 16)
            sp.dma_start(w2_sb[:], w2_t).then_inc(w2_in, 16)
            sp.dma_start(wt1[:], w_top1[0:2 * P].rearrange("(c p) n -> p c n", p=P)).then_inc(mlp_in, 16)
            sp.dma_start(wt1_d[:], w_top1[2 * P:]).then_inc(mlp_in, 16)
            sp.dma_start(wt2[:], w_top2.rearrange("(c p) n -> p c n", p=P)).then_inc(mlp_in, 16)
            sp.dma_start(dense[:], dense_t).then_inc(mlp_in, 16)
            sp.wait_ge(y_ready, NQ)
            sp.dma_start(y.rearrange("b o -> o b"), y_sb[:]).then_inc(stored, 16)
            sp.wait_ge(stored, 16)

        @block.gpsimd
        def _(pool):
            nc.gpsimd.memset(ident[:], 0.0).then_inc(ident_cleared, 1)
            pool.wait_ge(ident_cleared, 1)
            nc.gpsimd.affine_select(out=ident[:], in_=ident[:], compare_op=ALU.not_equal, fill=1.0, base=0,
                                    pattern=[[-1, P]], channel_multiplier=1).then_inc(ident_made, 1)
            pool.wait_ge(ids_in, 16)
            for q in range(NQ):
                if q >= 2:
                    pool.wait_ge(emb_turned, 2 * (q - 1))
                for f in range(F):
                    nc.gpsimd.indirect_dma_start(
                        out=emb[:, q % 2, f * K:(f + 1) * K], out_offset=None, in_=tables[f],
                        in_offset=bass.IndirectOffsetOnAxis(ap=idx[:, q, f:f + 1].bitcast(U32), axis=0),
                    ).then_inc(gathered[q][f >= A0], 16)

        @block.tensor
        def _(pe):
            pe.wait_ge(pairs_built, 1)
            pe.wait_ge(w2_in, 16)
            for l in range(F):
                if l >= 4:
                    pe.wait_ge(v_out_act if l % 2 == 0 else v_out_dve, (l - 4) // 2 + 1)
                nc.tensor.matmul(bank[l % 4][:, 0:NCOL], w2_sb[:, l, :], w1_pairs[:, :],
                                 start=True, stop=True).then_inc(v_filled, 1)
            pe.wait_ge(v_out_act, F // 2)
            pe.wait_ge(v_out_dve, F // 2)

            def columns_of(t):
                return diag[:, t].rearrange("p l g -> p (l g)")

            def triple_sums(q, half):
                pe.wait_ge(prod_ready, 2 * q + half + 1)
                pe.wait_ge(diag_ready, 4 * q + 3 + half)
                for t0 in range(half * HALF, (half + 1) * HALF, G1):
                    n1, n2 = q * T1 + t0 // G1, q * T2 + t0 // G2
                    if n1 >= 4:
                        pe.wait_ge(sum1_out, n1 - 3)
                    if t0 % G2 == 0 and n2 >= 2:
                        pe.wait_ge(sum2_out, n2 - 1)
                    for t in range(t0, t0 + G1):
                        o = t % G1 * NS1
                        mm = nc.tensor.matmul(sum1_banks[n1 % 4][:, o:o + NS1], prod[:, t, 0:P], columns_of(t),
                                              start=True, stop=True)
                    mm.then_inc(sum1_filled, 1)
                    for t in range(t0, t0 + G1):
                        o = t % G2 * NS2
                        mm = nc.tensor.matmul(sum2_banks[n2 % 2][0:NS, o:o + NS2], prod[:, t, P:NP],
                                              columns_of(t)[:, NG * L2:], start=True, stop=True)
                    if t % G2 == G2 - 1:
                        mm.then_inc(sum2_filled, 1)

            def turn_weights():
                pe.wait_ge(sum1_out, T1)
                pe.wait_ge(ident_made, 1)
                pe.wait_ge(cross_built, 1)
                pe.wait_ge(v_folded, 3)
                for n, (sources, _, _) in enumerate(turns):
                    if n >= 4:
                        pe.wait_ge(turned_out, n - 3)
                    for i, src in enumerate(sources):
                        mm = nc.tensor.transpose(bank[n % 4][0:src.shape[1], i * P:(i + 1) * P], src, ident[:])
                    mm.then_inc(turned_filled, 1)
                pe.wait_ge(turned_out, len(turns))

            def cin_maps(q):
                z2, z1 = z_bank[:, 0:P], z_bank[:, P:2 * P]
                pe.wait_ge(sum1_out, (q + 1) * T1)
                for l in range(F):
                    nc.tensor.matmul(z2, wgt1[:, 1 + CB + l, :], sums1[:, l, :], start=(l == 0), stop=False)
                pe.wait_ge(sum2_out, (q + 1) * T2)
                for l in range(NL2):
                    nc.tensor.matmul(z2, wgt2[:, 2 + l, :], sums2[:, l, :], start=False, stop=False)
                nc.tensor.matmul(z2, wgt2[:, 1, :], sums2[:, NL2, :], start=False, stop=True)
                nc.tensor.matmul(z1, wgt1[:, 0, :], sums1[:, F, :], start=True, stop=False)
                nc.tensor.matmul(z1, wgt2[:, 0, :], sums2[:, NL2, :], start=False, stop=False)
                pe.wait_ge(cross_ready, q + 1)
                for c in range(CB):
                    mm = nc.tensor.matmul(z1, wgt1[:, 1 + c, :], cross[:, c, :], start=False, stop=(c == CB - 1))
                mm.then_inc(z_filled, 1)

            def mlp_first(q):
                if q == 0:
                    pe.wait_ge(mlp_in, 16 * 4)
                pe.wait_ge(z_ready, q + 1)
                if q:
                    pe.wait_ge(y_ready, q)
                for m in range(M1):
                    cols = slice(m * P, (m + 1) * P)
                    nc.tensor.matmul(mlp_bank[:, cols], wt1_d[:, cols], dense[:, q, :], start=True, stop=False)
                    nc.tensor.matmul(mlp_bank[:, cols], wt1[:, 0, cols], z_sb[:, 0, :], start=False, stop=False)
                    mm = nc.tensor.matmul(mlp_bank[:, cols], wt1[:, 1, cols], z_sb[:, 1, :], start=False, stop=True)
                mm.then_inc(h1_filled, 1)

            def mlp_second(q):
                pe.wait_ge(h1_ready, q + 1)
                for m in range(M2):
                    for c in range(M1):
                        mm = nc.tensor.matmul(z_bank[:, (2 + m) * P:(3 + m) * P], wt2[:, c, m * P:(m + 1) * P],
                                              h1_sb[:, c, :], start=(c == 0), stop=(c == M1 - 1))
                mm.then_inc(h2_filled, 1)

            def mlp_third(q):
                pe.wait_ge(h2_ready, q + 1)
                for c in range(M2):
                    mm = nc.tensor.matmul(mlp_bank[0:1, 0:P], wt3[:, c:c + 1], h2_sb[:, c, :],
                                          start=(c == 0), stop=(c == M2 - 1))
                mm.then_inc(y_filled, 1)

            for q in range(NQ):
                triple_sums(q, 0)
                if q:
                    mlp_first(q - 1)
                triple_sums(q, 1)
                if q:
                    mlp_second(q - 1)
                    mlp_third(q - 1)
                else:
                    turn_weights()
                cin_maps(q)
            mlp_first(NQ - 1)
            mlp_second(NQ - 1)
            mlp_third(NQ - 1)

        @block.scalar
        def _(act):
            for l in range(0, F, 2):
                act.wait_ge(v_filled, l + 1)
                nc.scalar.activation(vmat[:, l, :], bank[l % 4][:, 0:NCOL], ACT.Copy).then_inc(v_out_act, 1)

            def diagonal(q, part, half):
                if q and part == 0:
                    act.wait_ge(sum2_filled, half_used(q - 1, half))
                f0, n = PARTS[part]
                ts = slice(half * HALF, (half + 1) * HALF)
                for g in range(NG):
                    rows = slice(g * SQ, (g + 1) * SQ)
                    nc.scalar.activation(diag[rows, ts, f0:f0 + n, g],
                                         emb_t[rows, q % 2, f0:f0 + n, ts].rearrange("p f t -> p t f"), ACT.Copy)
                nc.scalar.activation(prod[:, ts, P + f0:P + f0 + n],
                                     emb_t[:, q % 2, f0:f0 + n, ts].rearrange("p f t -> p t f"),
                                     ACT.Copy).then_inc(diag_ready, 1)

            def diagonals(q):
                for part in range(2):
                    act.wait_ge(emb_turned, 2 * q + part + 1)
                    for half in range(2):
                        diagonal(q, part, half)

            def copy_sums(q, half):
                if q and half == 0:
                    act.wait_ge(z_filled, q)
                for n in range(half * T1 // 2, (half + 1) * T1 // 2):
                    act.wait_ge(sum1_filled, q * T1 + n + 1)
                    nc.scalar.activation(in_sbuf(sums1, n, G1), in_psum(sum1_banks[n % 4], G1, NS1),
                                         ACT.Copy).then_inc(sum1_out, 1)
                    if n % 2:
                        m = n // 2
                        act.wait_ge(sum2_filled, q * T2 + m + 1)
                        nc.scalar.activation(in_sbuf(sums2, m, G2), in_psum(sum2_banks[m % 2][0:NS], G2, NS2),
                                             ACT.Copy).then_inc(sum2_out, 1)

            def relu(out, src, bias, filled, ready, q):
                act.wait_ge(filled, q + 1)
                for m in range(bias.shape[1]):
                    last = nc.scalar.activation(out[:, m, :], src[:, m * P:(m + 1) * P], ACT.Relu,
                                                bias=bias[:, m:m + 1])
                last.then_inc(ready, 1)

            def mlp_last(q):
                relu(h2_sb, z_bank[:, 2 * P:4 * P], bt2, h2_filled, h2_ready, q)
                act.wait_ge(y_filled, q + 1)
                nc.scalar.activation(y_sb[:, q * P:(q + 1) * P].rearrange("o (g t) -> o t g", g=NG),
                                     mlp_bank[0:1, 0:P].rearrange("o (t g) -> o t g", g=NG),
                                     ACT.Copy).then_inc(y_ready, 1)

            act.wait_ge(cleared, 3)
            act.wait_ge(v_filled, F)
            diagonals(0)
            for q in range(NQ):
                copy_sums(q, 0)
                if q:
                    relu(h1_sb, mlp_bank, bt1, h1_filled, h1_ready, q - 1)
                copy_sums(q, 1)
                if q:
                    mlp_last(q - 1)
                else:
                    for n, (sources, wgt, i) in enumerate(turns):
                        act.wait_ge(turned_filled, n + 1)
                        rows, cols = sources[0].shape[1], len(sources)
                        nc.scalar.activation(wgt[0:rows, i:i + cols, :].rearrange("p i h -> p (i h)"),
                                             bank[n % 4][0:rows, 0:cols * P], ACT.Copy).then_inc(turned_out, 1)
                if q + 1 < NQ:
                    diagonals(q + 1)
                act.wait_ge(z_filled, q + 1)
                nc.scalar.activation(z_sb[:, 0, :], z_bank[:, P:2 * P], ACT.Identity, bias=kbias[:, 0:1])
                nc.scalar.activation(z_sb[:, 1, :], z_bank[:, 0:P], ACT.Identity,
                                     bias=kbias[:, 1:2]).then_inc(z_ready, 1)
            relu(h1_sb, mlp_bank, bt1, h1_filled, h1_ready, NQ - 1)
            mlp_last(NQ - 1)

        @block.vector
        def _(dve):
            nc.vector.memset(w1_pairs[:, GAP:SB], 0.0)
            nc.vector.memset(w1_cross[:], 0.0).then_inc(cleared, 1)
            dve.wait_ge(cin_in, 32)
            eye = w1_sb[:].rearrange("p a b -> p (a b)")[:, 0:F * F:F + 1]
            nc.vector.tensor_scalar(eye, eye, 0.5, None, ALU.mult).then_inc(halved, 1)
            dve.wait_ge(halved, 1)
            for c, (f0, n) in enumerate(CLIQUES):
                for j in range(n):
                    o = START[c] + j * (j + 1) // 2
                    nc.vector.tensor_tensor(w1_pairs[:, o:o + j + 1], w1_sb[:, f0:f0 + j + 1, f0 + j],
                                            w1_sb[:, f0 + j, f0:f0 + j + 1], ALU.add)
            for o, u0, nu, v0, nv in ((XB, 0, A0, A0, C3), (SB, 0, C0, C0, C1 + C2), (RB, C0, C1, L2, C2)):
                nc.vector.tensor_tensor(
                    w1_pairs[:, o:o + nu * nv].rearrange("p (u v) -> p u v", v=nv),
                    w1_sb[:, u0:u0 + nu, v0:v0 + nv],
                    w1_sb[:, v0:v0 + nv, u0:u0 + nu].rearrange("p v u -> p u v"), ALU.add)
            nc.vector.tensor_copy(w1_pairs[:, UB:NCOL], cols_sb[:, 0:1]).then_inc(pairs_built, 1)
            nc.vector.tensor_scalar(kbias[:], b12, float(K), None, ALU.mult)
            nc.vector.memset(diag[:], 0.0)
            nc.vector.memset(cross[:], 0.0)
            nc.vector.memset(u_pad[:], 0.0).then_inc(cleared, 1)
            dve.wait_ge(cleared, 2)
            for g in range(NG):
                last = nc.vector.memset(diag[g * SQ:(g + 1) * SQ, :, F, g], 1.0)
            last.then_inc(cleared, 1)

            dve.wait_ge(pairs_built, 1)
            for a in range(C3):
                last = nc.vector.tensor_copy(w1_cross[:, a % CB, a // CB * SQ:a // CB * SQ + A0],
                                             w1_pairs[:, XB + a:GAP:C3])
            last.then_inc(cross_built, 1)

            for l in range(1, F, 2):
                dve.wait_ge(v_filled, l + 1)
                nc.vector.tensor_copy(vmat[:, l, :], bank[l % 4][:, 0:NCOL]).then_inc(v_out_dve, 1)

            def fold_v():
                dve.wait_ge(v_out_act, F // 2)
                dve.wait_ge(v_out_dve, F // 2)
                x = vmat[:, :, XB:GAP].rearrange("p l (u a) -> p l u a", a=C3)
                s_ = vmat[:, :, SB:RB].rearrange("p l (u v) -> p l u v", v=C1 + C2)
                r = vmat[:, :, RB:UB]
                nc.vector.tensor_copy(u_pad[:, 0:F], vmat[:, :, UB]).then_inc(v_folded, 1)

                def add(dst, term):
                    return nc.vector.tensor_tensor(dst, dst, term, ALU.add)

                for second in range(2):
                    for c, (f0, n) in enumerate(CLIQUES):
                        for j in range(n):
                            m = j if second else j + 1
                            if m == 0:
                                continue
                            o = START[c] + j * (j + 1) // 2

                            def term(pairs):
                                if second:
                                    return pairs[:, f0:f0 + m, j, :].rearrange("p i v -> p v i")
                                return pairs[:, f0 + j, 0:m, :].rearrange("p i v -> p v i")
                            if c == 3:
                                t3 = x[:, f0:f0 + m, :, j].rearrange("p i u -> p u i") if second else x[:, f0 + j, :, 0:m]
                                add(vmat[:, 0:A0, o:o + m], t3)
                            else:
                                add(vmat[:, A0:F, o:o + m], term(x[:, :, f0:f0 + n]))
                            if c == 0:
                                add(vmat[:, C0:A0, o:o + m], term(s_))
                            if c == 1:
                                t1 = s_[:, f0:f0 + m, :, j].rearrange("p i u -> p u i") if second else s_[:, f0 + j, :, 0:m]
                                add(vmat[:, 0:C0, o:o + m], t1)
                                t2 = r[:, f0:f0 + m, j] if second else r[:, f0 + j, 0:m]
                                add(vmat[:, L2, o:o + m], t2)
                    for v in range(C1 + C2):
                        dst = vmat[:, A0:F, SB + v:RB:C1 + C2]
                        if second:
                            add(dst, x[:, 0:C0, C0 + v, :].rearrange("p u a -> p a u"))
                        else:
                            add(dst, x[:, C0 + v, 0:C0, :].rearrange("p u a -> p a u"))
                    dst = vmat[:, A0:F, RB:UB]
                    last = add(dst, x[:, C0:L2, L2, :].rearrange("p v a -> p a v") if second
                               else x[:, L2, C0:L2, :].rearrange("p v a -> p a v"))
                    dst = s_[:, L2, :, 0:C1]
                    last = add(dst, r[:, 0:C0, :] if second
                               else s_[:, C0:L2, :, C1].rearrange("p v u -> p u v"))
                    last.then_inc(v_folded, 1)
                    if not second:
                        dve.wait_ge(v_folded, 2)

            def products(q, part, half):
                if q and part == 0:
                    dve.wait_ge(sum2_filled, half_used(q - 1, half))
                et = emb_t[:, q % 2]
                ts = slice(half * HALF, (half + 1) * HALF)

                def fields(a, n, clique=1):
                    return bass.AP(et.tensor, et.offset + a * SQ + half * HALF,
                                   [list(et.ap[0]), [1, HALF], [C0 * SQ, clique], [SQ, n]])

                def one_field(a, n, clique=1):
                    return bass.AP(et.tensor, et.offset + a * SQ + half * HALF,
                                   [list(et.ap[0]), [1, HALF], [C0 * SQ, clique], [0, n]])

                def place(o, n, clique=1):
                    p0 = prod[:, ts]
                    return bass.AP(p0.tensor, p0.offset + o, [list(p0.ap[0]), [NP, HALF], [START[1], clique], [1, n]])

                for c, j0, together in (((0, 0, 2), (0, C1, 1), (2, 0, 1)), ((3, 0, 1),))[part]:
                    f0, n = CLIQUES[c]
                    for j in range(j0, C1 if together == 2 else n):
                        o = START[c] + j * (j + 1) // 2
                        last = nc.vector.tensor_tensor(place(o, j + 1, together), fields(f0, j + 1, together),
                                                       one_field(f0 + j, j + 1, together), ALU.mult)
                if part == 1:
                    last.then_inc(prod_ready, 1)
                    return
                o, nv = P + F, C1 + C2
                u_of = bass.AP(et.tensor, et.offset + half * HALF, [list(et.ap[0]), [1, HALF], [SQ, C0], [0, nv]])
                v_of = bass.AP(et.tensor, et.offset + C0 * SQ + half * HALF,
                               [list(et.ap[0]), [1, HALF], [0, C0], [SQ, nv]])
                nc.vector.tensor_tensor(prod[:, ts, o:o + C0 * nv].rearrange("p t (u v) -> p t u v", v=nv),
                                        u_of, v_of, ALU.mult)
                nc.vector.tensor_tensor(place(o + C0 * nv, C1), fields(C0, C1), one_field(L2, C1), ALU.mult)

            for q in range(NQ):
                for part, (f0, n) in enumerate(PARTS):
                    dve.wait_ge(gathered[q][part], 16 * n)
                    if q >= 2:
                        dve.wait_ge(diag_ready, 4 * (q - 1))
                    nc.vector.transpose(emb_t[:, q % 2, f0:f0 + n].rearrange("p f t -> p (f t)"),
                                        emb[:, q % 2, f0 * K:(f0 + n) * K]).then_inc(emb_turned, 1)
                    dve.wait_ge(emb_turned, 2 * q + part + 1)
                    if q == 0:
                        dve.wait_ge(v_filled, F)
                    products(q, part, 0)
                    products(q, part, 1)
                if q == 0:
                    fold_v()

                dve.wait_ge(sum2_out, (q + 1) * T2)
                if q:
                    dve.wait_ge(z_filled, q)
                for g in range(NG):
                    a = A0 - L2 + CB * g
                    last = nc.vector.tensor_copy(cross[g * SQ:g * SQ + A0, :, :], sums2[0:A0, a:a + CB, :])
                last.then_inc(cross_ready, 1)


def kernel(**inputs):
    import numpy as np
    import concourse.bacc as bacc
    from concourse.bass_utils import run_bass_kernel_spmd as run

    nc = bacc.Bacc("TRN2", target_bir_lowering=False, num_devices=1)
    arrays = {}

    def give(name, a):
        a = np.ascontiguousarray(a)
        arrays["in_" + name] = a
        return nc.dram_tensor("in_" + name, a.shape, mybir.dt.from_np(a.dtype), kind="ExternalInput").ap()

    ids = give("ids", inputs["ids"])
    tables = [give(f"tbl_{f}", inputs[f"tbl_{f}"]) for f in range(F)]
    dense_t = give("dense_t", np.asarray(inputs["dense_ctx"]).reshape(NQ, NG, SQ, ND).transpose(3, 0, 2, 1)
                   .reshape(ND, NQ, P))
    w1 = give("w1", inputs["L0_rec_W1"])
    w2_t = give("w2_t", np.asarray(inputs["L0_rec_W2"]).transpose(1, 2, 0))
    vectors = [np.asarray(inputs[n]).reshape(-1, P) for n in ("L0_rec_b1", "L0_rec_b2", "b_top1", "b_top2", "W_top3")]
    columns = give("columns", np.concatenate(vectors).T)
    y = nc.dram_tensor("out_y", (B, 1), F32, kind="ExternalOutput").ap()
    build(nc, ids, tables, dense_t, w1, w2_t, columns, give("W_top1", inputs["W_top1"]),
          give("W_top2", inputs["W_top2"]), y)
    r = run(nc, [arrays], core_ids=[0])
    return r.results[0]["out_y"]
```

```python
from contextlib import ExitStack

import concourse.bass as bass
from concourse import mybir

F32 = mybir.dt.float32
I32 = mybir.dt.int32
U32 = mybir.dt.uint32
ALU = mybir.AluOpType
ACT = mybir.ActivationFunctionType
AX = mybir.AxisListType

P = 128
SQ = 32
B, F, K, H = 512, 26, 32, 128
NQ = B // P
NG = P // SQ
ND, N1, N2 = 16, 512, 256
M1, M2 = N1 // P, N2 // P

CLIQUES = [(0, 7), (7, 6), (13, 1), (14, 12)]
START = [0]
for _, n in CLIQUES:
    START.append(START[-1] + n * (n + 1) // 2)
LIST1 = START[-1]


def pair_col(c, j):
    return START[c] + j * (j - 1) // 2


def square_col(c):
    return pair_col(c, CLIQUES[c][1])


C0, C1, C2, C3 = (n for _, n in CLIQUES)
L2 = C0 + C1
NL2 = F - L2
A0 = L2 + C2
SB = 0
RB = SB + C0 * (C1 + C2)
LB = RB + C1 * C2
XB = LB + LIST1
UB = XB + A0 * C3
NCOL = UB + 1
LIST2 = LB - SB
NP = P + LIST2
NU, UP = (NL2 + 1) // 2, 64
assert NL2 + 1 == 2 * NU and LIST2 <= UP
assert LIST1 == P and LIST1 + A0 * C3 + LIST2 == F * (F + 1) // 2

NS1 = (F + 1) * NG
NS2 = (NL2 + 1) * NG
PARTS = ((0, A0), (A0, C3 - 3), (F - 3, 3))
NPART = len(PARTS)
OF, NF, ROWS, RP = A0, 2, 1000, 8
NA = ROWS // RP
FETCH_AHEAD = 7
assert NA * RP == ROWS and NA <= P
GATHERED = [[f for f in range(f0, f0 + n) if not OF <= f < OF + NF] for f0, n in PARTS]
HALF = SQ // 2
STEPS = [((0, SQ),)] * (NPART - 1) + [((0, HALF), (HALF, SQ))]
ND_TILE = sum(len(s) for s in STEPS)
G1, G2 = 4, 8
NX = A0 * C3
GS = NX - P + -(NX - P) % SQ
GW = GS + F
UH = A0 // 2


def build(nc, ids, ids_of, marks, tables, dense_t, w1, w2_t, columns, w_top1, w_top2, y):
    with ExitStack() as ctx:
        def sb(name, shape, dt=F32):
            return ctx.enter_context(nc.sbuf_tensor(name, shape, dt))

        def sem(name):
            return ctx.enter_context(nc.semaphore(name))

        idx = sb("idx", [P, NQ, F], I32)
        emb = sb("emb", [P, 2, F * K])
        ids_row = sb("ids_row", [NA, NF * B], I32)
        ids_f = sb("ids_f", [NA, NF * B])
        from_first = sb("from_first", [NA, NF * B])
        hot = sb("hot", [NA, NF * B])
        marks_sb = sb("marks_sb", [P, 2 + RP])
        low_id = sb("low_id", [P, NF, NQ])
        low_f, quot, quot_big, quot_8 = (sb(n, [P, NF, NQ]) for n in ("low_f", "quot", "quot_big", "quot_8"))
        mask = sb("mask", [P, NF, NQ, RP])
        table_sb = sb("table_sb", [NA, NF, RP * K])
        masked = sb("masked", [P, NF, NQ, RP, K])
        fetched = sb("fetched", [P, NQ, NF, K])
        emb_t = sb("emb_t", [P, 2, F, SQ])
        prod = sb("prod", [P, SQ, NP])
        diag = sb("diag", [P, SQ, F + 1, NG])
        sums1 = sb("sums1", [P, F + 1, P])
        w2_sb = sums1[:, 0:F]
        sums2 = sb("sums2", [UP + LIST2, NU, P])
        cross = sb("cross", [P, 2, UH, C3, K])
        gram = sb("gram", [P, P + GW])
        gram_t = sb("gram_t", [P, 2, P])
        ident = sb("ident", [P, P])
        w1_sb = sb("w1_sb", [P, F, F])
        w1_pairs = sb("w1_pairs", [P, NCOL])
        vmat = sb("vmat", [P, F, NCOL])
        block2 = sb("block2", [P, 2, GW])
        wgt1 = sb("wgt1", [P, 2 + F, P])
        wgt2 = sb("wgt2", [UP + LIST2, NU + 1, P])
        wgt3 = sb("wgt3", [GW, 2, P])
        cols_sb = sb("cols_sb", [P, 2 + M1 + 2 * M2])
        b12 = cols_sb[:, 0:2]
        bt1 = cols_sb[:, 2:2 + M1]
        bt2 = cols_sb[:, 2 + M1:2 + M1 + M2]
        wt3 = cols_sb[:, 2 + M1 + M2:]
        kbias = sb("kbias", [P, 2])
        wt1 = sb("wt1", [P, 2, N1])
        wt1_d = sb("wt1_d", [ND, N1])
        wt2 = sb("wt2", [P, M1, N2])
        dense = sb("dense", [ND, NQ, P])
        z_sb = sb("z_sb", [P, 2, P])
        dense_h = sb("dense_h", [P, M1, B])
        h1_pre = sb("h1_pre", [P, M1, P])
        h1_sb = sb("h1_sb", [P, M1, P])
        h2_sb = sb("h2_sb", [P, M2, P])
        y_sb = sb("y_sb", [1, B])

        bank = [ctx.enter_context(nc.psum_tensor(f"bank{i}", [P, 512], F32)) for i in range(8)]
        sum1_banks, h2_bank, sum2_banks = bank[0:3], bank[3], bank[4:6]
        z_bank, mlp_bank = bank[6], bank[7]
        dense_banks = (bank[3], z_bank, mlp_bank, sum2_banks[1])

        ids_in = sem("ids_in")
        cin_in = sem("cin_in")
        w2_in = [sem(f"w2_in{i}") for i in range(2)]
        mlp_in = sem("mlp_in")
        gathered = [[sem(f"gathered{q}_{part}") for part in range(NPART)] for q in range(NQ)]
        hot_in = sem("hot_in")
        hot_steps = sem("hot_steps")
        hot_ready = sem("hot_ready")
        mask_steps = sem("mask_steps")
        candidates_filled = sem("candidates_filled")
        masked_ready = sem("masked_ready")
        fetch_done = sem("fetch_done")
        placed = sem("placed")
        ident_cleared = sem("ident_cleared")
        ident_made = sem("ident_made")
        cleared = sem("cleared")
        pairs_built = sem("pairs_built")
        v_filled = sem("v_filled")
        v_out = sem("v_out")
        v_folded = sem("v_folded")
        turned_filled = sem("turned_filled")
        turned_out = sem("turned_out")
        emb_turned = sem("emb_turned")
        prod_ready = sem("prod_ready")
        diag_ready = sem("diag_ready")
        sum1_filled = sem("sum1_filled")
        sum1_out = sem("sum1_out")
        sum2_filled = sem("sum2_filled")
        sum2_out = sem("sum2_out")
        crossed = sem("crossed")
        fields_summed = sem("fields_summed")
        gram_ready = sem("gram_ready")
        gram_filled = sem("gram_filled")
        gram_out = sem("gram_out")
        dense_filled = sem("dense_filled")
        dense_out = sem("dense_out")
        sums_used = sem("sums_used")
        z_filled = sem("z_filled")
        z_ready = sem("z_ready")
        h1_filled = sem("h1_filled")
        h1_summed = sem("h1_summed")
        h1_ready = sem("h1_ready")
        h2_filled = sem("h2_filled")
        h2_ready = sem("h2_ready")
        h2_last_ready = sem("h2_last_ready")
        z1_last_filled = sem("z1_last_filled")
        z1_last_ready = sem("z1_last_ready")
        y_filled = sem("y_filled")
        y_ready = sem("y_ready")
        stored = sem("stored")

        block = ctx.enter_context(nc.Block())

        one = [w1_pairs[:, LB:XB], w1_pairs[:, XB:XB + P]] + [vmat[:, l, LB:XB] for l in range(F)]
        two = [vmat[:, L2 + l, SB:LB] for l in range(NL2)] + [w1_pairs[:, SB:LB]]
        three = [block2[:, i, :] for i in range(2)]
        turns = [(sources[i:i + 4], wgt, r0, o + i)
                 for sources, wgt, r0, o in ((one, wgt1, 0, 0), (two[:NU], wgt2, 0, 0), (two[NU:-1], wgt2, UP, 0),
                                             (two[-1:], wgt2, UP, NU), (three, wgt3, 0, 0))
                 for i in range(0, len(sources), 4)]
        T1, T2 = SQ // G1, SQ // G2

        def in_psum(src, steps, width):
            return src[:, 0:steps * width].rearrange("p (t l g) -> p l t g", t=steps, g=NG)

        def in_sbuf(dst, n, steps):
            return dst[:, :, n * steps * NG:(n + 1) * steps * NG].rearrange("p l (t g) -> p l t g", g=NG)

        def z1_out(q):
            return bank[5][:, 0:P] if q == NQ - 1 else h2_bank[:, M2 * P:(M2 + 1) * P]

        def candidates(f, i):
            return bank[4 + 2 * f + i][:, 0:2 * RP * K].rearrange("p (q n) -> p q n", q=2)

        def gram_bank(q):
            return bank[0] if q == NQ - 1 else mlp_bank

        def y_out(q):
            return (z_bank if q == NQ - 1 else mlp_bank)[0:1, 0:P]

        def h1_out(q, m):
            return bank[m][:, 0:P] if q == NQ - 1 else mlp_bank[:, m * P:(m + 1) * P]

        def h2_out(q, m):
            return bank[4 + m][:, 0:P] if q == NQ - 1 else h2_bank[:, m * P:(m + 1) * P]

        @block.sync
        def _(sp):
            sp.dma_start(idx[:], ids.rearrange("(q p) f -> p q f", p=P)).then_inc(ids_in, 16)
            sp.dma_start(w1_sb[:], w1).then_inc(cin_in, 16)
            sp.dma_start(cols_sb[:], columns).then_inc(cin_in, 16)
            for i in range(2):
                ls = slice(i * F // 2, (i + 1) * F // 2)
                sp.dma_start(w2_sb[:, ls], w2_t[:, ls]).then_inc(w2_in[i], 16)
            sp.dma_start(ids_row[:], bass.AP(ids_of.tensor, ids_of.offset, [[0, NA], [1, NF * B]])).then_inc(hot_in, 16)
            sp.dma_start(marks_sb[:], marks).then_inc(hot_in, 16)
            for f in range(NF):
                sp.dma_start(table_sb[:, f], tables[OF + f].rearrange("(a b) k -> a (b k)", b=RP)).then_inc(hot_in, 16)
            sp.dma_start(wt1[:], w_top1[0:2 * P].rearrange("(c p) n -> p c n", p=P)).then_inc(mlp_in, 16)
            sp.dma_start(wt1_d[:], w_top1[2 * P:]).then_inc(mlp_in, 16)
            sp.dma_start(wt2[:], w_top2.rearrange("(c p) n -> p c n", p=P)).then_inc(mlp_in, 16)
            sp.dma_start(dense[:], dense_t).then_inc(mlp_in, 16)
            sp.wait_ge(y_ready, NQ)
            sp.dma_start(y.rearrange("b o -> o b"), y_sb[:]).then_inc(stored, 16)
            sp.wait_ge(stored, 16)

        @block.gpsimd
        def _(pool):
            nc.gpsimd.memset(ident[:], 0.0).then_inc(ident_cleared, 1)
            pool.wait_ge(ident_cleared, 1)
            nc.gpsimd.affine_select(out=ident[:], in_=ident[:], compare_op=ALU.not_equal, fill=1.0, base=0,
                                    pattern=[[-1, P]], channel_multiplier=1).then_inc(ident_made, 1)
            pool.wait_ge(ids_in, 16)
            for q in range(NQ):
                if q >= 2:
                    pool.wait_ge(emb_turned, NPART * (q - 1))
                    pool.wait_ge(fields_summed, q - 1)
                for part, fields in enumerate(GATHERED):
                    for f in fields:
                        nc.gpsimd.indirect_dma_start(
                            out=emb[:, q % 2, f * K:(f + 1) * K], out_offset=None, in_=tables[f],
                            in_offset=bass.IndirectOffsetOnAxis(ap=idx[:, q, f:f + 1].bitcast(U32), axis=0),
                        ).then_inc(gathered[q][part], 16)

        @block.tensor
        def _(pe):
            pe.wait_ge(pairs_built, 1)
            pe.wait_ge(w2_in[0], 16)
            for l in range(F):
                if l == F // 2:
                    pe.wait_ge(w2_in[1], 16)
                if l == F - FETCH_AHEAD:
                    pe.wait_ge(hot_in, 16 * (2 + NF))
                    pe.wait_ge(hot_ready, 1)
                    for f in range(NF):
                        for q in range(NQ):
                            o = f * B + q * P
                            mm = nc.tensor.matmul(candidates(f, q // 2)[:, q % 2], hot[:, o:o + P], table_sb[:, f],
                                                  start=True, stop=True)
                    mm.then_inc(candidates_filled, 1)
                if l >= 4:
                    pe.wait_ge(v_out, l - 3)
                nc.tensor.matmul(bank[l % 4][:, SB:NCOL], w2_sb[:, l, :], w1_pairs[:, SB:],
                                 start=True, stop=True).then_inc(v_filled, 1)
            pe.wait_ge(mlp_in, 16 * 4)
            pe.wait_ge(masked_ready, 1)
            pe.wait_ge(v_out, F - 2)
            for m in range(M1):
                nc.tensor.matmul(dense_banks[m][:, 0:B], wt1_d[:, m * P:(m + 1) * P],
                                 dense[:].rearrange("p q c -> p (q c)"), start=True, stop=True).then_inc(dense_filled, 1)
            pe.wait_ge(v_out, F)

            def columns_of(t):
                return diag[:, t].rearrange("p l g -> p (l g)")

            def triple_sums(q, quarter, between=None):
                if quarter % 2 == 0:
                    half = quarter // 2
                    pe.wait_ge(prod_ready, 2 * q + half + 1)
                    pe.wait_ge(diag_ready, (q + 1) * ND_TILE - 1 + half)
                n2 = q * T2 + quarter
                if n2 >= 2:
                    pe.wait_ge(sum2_out, n2 - 1)
                for t0 in range(quarter * G2, (quarter + 1) * G2, G1):
                    n1 = q * T1 + t0 // G1
                    if n1 >= 3:
                        pe.wait_ge(sum1_out, n1 - 2)
                    if n1 == 2:
                        pe.wait_ge(dense_out, M1)
                    for t in range(t0, t0 + G1):
                        o = t % G1 * NS1
                        mm = nc.tensor.matmul(sum1_banks[n1 % 3][:, o:o + NS1], prod[:, t, 0:P], columns_of(t),
                                              start=True, stop=True)
                    mm.then_inc(sum1_filled, 1)
                    for t in range(t0, t0 + G1):
                        o = t % G2 * NS2
                        mm = nc.tensor.matmul(sum2_banks[n2 % 2][0:LIST2, o:o + NS2], prod[:, t, P:NP],
                                              columns_of(t)[:, NG * L2:], start=True, stop=True)
                    if between and t < (quarter + 1) * G2 - 1:
                        between()
                mm.then_inc(sum2_filled, 1)

            def turn_weights():
                pe.wait_ge(sum1_out, T1)
                pe.wait_ge(ident_made, 1)
                pe.wait_ge(v_folded, 3)
                for n, (sources, _, _, _) in enumerate(turns):
                    if n >= 4:
                        pe.wait_ge(turned_out, n - 3)
                    for i, src in enumerate(sources):
                        mm = nc.tensor.transpose(bank[n % 4][0:src.shape[1], i * P:(i + 1) * P], src, ident[:])
                    mm.then_inc(turned_filled, 1)

            def z2_list_one(q):
                pe.wait_ge(sum1_out, (q + 1) * T1)
                if q == 0:
                    pe.wait_ge(turned_out, -(-len(one) // 4))
                for l in range(F):
                    nc.tensor.matmul(z_bank[:, 0:P], wgt1[:, 2 + l, :], sums1[:, l, :], start=(l == 0), stop=False)

            def z2_list_two(q, places):
                if q == 0:
                    pe.wait_ge(turned_out, len(turns))
                pe.wait_ge(sum2_out, (q + 1) * T2)
                for i in places:
                    nc.tensor.matmul(z_bank[:, 0:P], wgt2[:, i, :], sums2[:, i, :], start=False, stop=False)

            def z1_lists(q):
                nc.tensor.matmul(z1_out(q), wgt1[:, 0, :], sums1[:, F, :], start=True, stop=False)
                return nc.tensor.matmul(z1_out(q), wgt2[:, NU, :], sums2[:, NU - 1, :], start=False, stop=False)

            def turn_gram(q):
                pe.wait_ge(gram_ready, q + 1)
                if 0 < q < NQ - 1:
                    pe.wait_ge(y_ready, q)
                nc.tensor.transpose(gram_bank(q)[:, 0:P], gram[:, 0:P], ident[:])
                nc.tensor.transpose(gram_bank(q)[0:GW, P:2 * P], gram[:, P:], ident[:]).then_inc(gram_filled, 1)

            def z1_gram(q):
                pe.wait_ge(gram_out, q + 1)
                nc.tensor.matmul(z1_out(q), wgt1[:, 1, :], gram_t[:, 0, :], start=False, stop=False)
                return nc.tensor.matmul(z1_out(q), wgt3[:, 0, :], gram_t[0:GW, 1, :], start=False, stop=True)

            def z2_fields(q):
                return nc.tensor.matmul(z_bank[:, 0:P], wgt3[:, 1, :], gram_t[0:GW, 1, :], start=False, stop=True)

            def z_end(q):
                z1_gram(q)
                z2_fields(q).then_inc(z_filled, 1)

            def mlp_first(q):
                pe.wait_ge(z_ready, q + 1)
                if q:
                    pe.wait_ge(y_ready, q)
                for m in range(M1):
                    out, cols = h1_out(q, m), slice(m * P, (m + 1) * P)
                    nc.tensor.matmul(out, wt1[:, 0, cols], z_sb[:, 0, :], start=True, stop=False)
                    mm = nc.tensor.matmul(out, wt1[:, 1, cols], z_sb[:, 1, :], start=False, stop=True)
                mm.then_inc(h1_filled, 1)

            def mlp_first_last():
                for c, ready, count in ((0, z1_last_ready, 1), (1, z_ready, NQ)):
                    pe.wait_ge(ready, count)
                    for m in range(M1):
                        mm = nc.tensor.matmul(h1_out(NQ - 1, m), wt1[:, c, m * P:(m + 1) * P], z_sb[:, c, :],
                                              start=(c == 0), stop=(c == 1))
                        if c == 1:
                            mm.then_inc(h1_filled, 1)

            def mlp_second(q):
                pe.wait_ge(h1_ready, q + 1)
                for m in range(M2):
                    for c in range(M1):
                        mm = nc.tensor.matmul(h2_out(q, m), wt2[:, c, m * P:(m + 1) * P],
                                              h1_sb[:, c, :], start=(c == 0), stop=(c == M1 - 1))
                mm.then_inc(h2_filled, 1)

            def mlp_second_last():
                for c in range(M1):
                    pe.wait_ge(h1_ready, NQ + c)
                    for m in range(M2):
                        mm = nc.tensor.matmul(h2_out(NQ - 1, m), wt2[:, c, m * P:(m + 1) * P],
                                              h1_sb[:, c, :], start=(c == 0), stop=(c == M1 - 1))
                        if c == M1 - 1:
                            mm.then_inc(h2_filled, 1)

            def mlp_third(q):
                pe.wait_ge(h2_ready, q + 1)
                if q == NQ - 1:
                    pe.wait_ge(h2_last_ready, 1)
                for c in range(M2):
                    mm = nc.tensor.matmul(y_out(q), wt3[:, c:c + 1], h2_sb[:, c, :],
                                          start=(c == 0), stop=(c == M2 - 1))
                mm.then_inc(y_filled, 1)

            for q in range(NQ):
                triple_sums(q, 0)
                triple_sums(q, 1)
                triple_sums(q, 2)
                if q:
                    turn_gram(q - 1)
                triple_sums(q, 3, between=(lambda: z_end(q - 1)) if q else None)
                if q:
                    mlp_first(q - 1)
                else:
                    turn_weights()
                z2_list_one(q)
                if q:
                    mlp_second(q - 1)
                if q < NQ - 1:
                    z2_list_two(q, range(NU))
                    if q:
                        mlp_third(q - 1)
                    z1_lists(q).then_inc(sums_used, 1)
            q = NQ - 1
            turn_gram(q)
            z2_list_two(q, range(NU // 2))
            z1_lists(q)
            z1_gram(q).then_inc(z1_last_filled, 1)
            z2_list_two(q, range(NU // 2, NU))
            z2_fields(q).then_inc(z_filled, 1)
            mlp_first_last()
            mlp_third(NQ - 2)
            mlp_second_last()
            mlp_third(NQ - 1)

        @block.scalar
        def _(act):
            def diagonal(q, part, t0, t1):
                if q and part == 0:
                    act.wait_ge(sum2_filled, q * T2)
                f0, n = PARTS[part]
                ts = slice(t0, t1)
                for g in range(NG):
                    rows = slice(g * SQ, (g + 1) * SQ)
                    nc.scalar.activation(diag[rows, ts, f0:f0 + n, g],
                                         emb_t[rows, q % 2, f0:f0 + n, ts].rearrange("p f t -> p t f"), ACT.Copy)
                for c, (c0, cn) in enumerate(CLIQUES):
                    a, b = max(c0, f0), min(c0 + cn, f0 + n)
                    if a < b:
                        o = square_col(c) + a - c0
                        last = nc.scalar.activation(prod[:, ts, o:o + b - a],
                                                    emb_t[:, q % 2, a:b, ts].rearrange("p f t -> p t f"), ACT.Square)
                last.then_inc(diag_ready, 1)

            def diagonals(q, part):
                act.wait_ge(emb_turned, NPART * q + part + 1)
                for t0, t1 in STEPS[part]:
                    diagonal(q, part, t0, t1)

            def copy_gram(q):
                act.wait_ge(gram_filled, q + 1)
                for i, rows in enumerate((P, GW)):
                    last = nc.scalar.activation(gram_t[0:rows, i, :].rearrange("p (t g) -> p g t", g=NG),
                                                gram_bank(q)[0:rows, i * P:(i + 1) * P].rearrange("p (g t) -> p g t", g=NG),
                                                ACT.Copy)
                last.then_inc(gram_out, 1)

            def copy_sum1(q, n):
                if q and n == 0:
                    act.wait_ge(sums_used, q)
                act.wait_ge(sum1_filled, q * T1 + n + 1)
                nc.scalar.activation(in_sbuf(sums1, n, G1), in_psum(sum1_banks[(q * T1 + n) % 3], G1, NS1),
                                     ACT.Copy).then_inc(sum1_out, 1)

            def copy_sum2(q, n):
                act.wait_ge(sum2_filled, q * T2 + n + 1)
                for i, r0 in enumerate((0, UP)):
                    last = nc.scalar.activation(
                        in_sbuf(sums2[r0:r0 + LIST2], n, G2),
                        in_psum(sum2_banks[n % 2][0:LIST2], G2, NS2)[:, i * NU:(i + 1) * NU], ACT.Copy)
                last.then_inc(sum2_out, 1)

            def relu_h1(q):
                act.wait_ge(h1_summed, q + 1)
                nc.scalar.activation(h1_sb[:], h1_pre[:], ACT.Relu).then_inc(h1_ready, 1)

            def relu_h2(q, blocks):
                for m in range(blocks):
                    last = nc.scalar.activation(h2_sb[:, m, :], h2_out(q, m), ACT.Relu, bias=bt2[:, m:m + 1])
                last.then_inc(h2_ready, 1)

            def copy_y(q):
                act.wait_ge(y_filled, q + 1)
                nc.scalar.activation(y_sb[:, q * P:(q + 1) * P].rearrange("o (g t) -> o t g", g=NG),
                                     y_out(q).rearrange("o (t g) -> o t g", g=NG),
                                     ACT.Copy).then_inc(y_ready, 1)

            def copy_z(q):
                act.wait_ge(z_filled, q + 1)
                nc.scalar.activation(z_sb[:, 0, :], z1_out(q), ACT.Identity, bias=kbias[:, 0:1])
                nc.scalar.activation(z_sb[:, 1, :], z_bank[:, 0:P], ACT.Identity,
                                     bias=kbias[:, 1:2]).then_inc(z_ready, 1)

            for l in range(F):
                act.wait_ge(v_filled, l + 1)
                nc.scalar.activation(vmat[:, l, SB:], bank[l % 4][:, SB:NCOL], ACT.Copy).then_inc(v_out, 1)
                if l == F - FETCH_AHEAD - 1:
                    act.wait_ge(cleared, 2)
                    diagonals(0, 0)
            for part in range(1, NPART):
                diagonals(0, part)
            act.wait_ge(mlp_in, 16 * 4)
            for m in range(M1):
                act.wait_ge(dense_filled, m + 1)
                nc.scalar.activation(dense_h[:, m, :], dense_banks[m][:, 0:B], ACT.Identity,
                                     bias=bt1[:, m:m + 1]).then_inc(dense_out, 1)

            for q in range(NQ):
                for n in range(T1):
                    copy_sum1(q, n)
                    if q and n == T1 - 2:
                        copy_z(q - 1)
                    if n % 2:
                        copy_sum2(q, n // 2)
                    if q and n == T1 - 3:
                        copy_gram(q - 1)
                if q:
                    relu_h1(q - 1)
                else:
                    for n, (sources, wgt, r0, i) in enumerate(turns):
                        act.wait_ge(turned_filled, n + 1)
                        rows, cols = sources[0].shape[1], len(sources)
                        nc.scalar.activation(wgt[r0:r0 + rows, i:i + cols, :].rearrange("p i h -> p (i h)"),
                                             bank[n % 4][0:rows, 0:cols * P], ACT.Copy).then_inc(turned_out, 1)
                if q + 1 < NQ:
                    for part in range(NPART - 1):
                        diagonals(q + 1, part)
                if q:
                    act.wait_ge(h2_filled, q)
                    relu_h2(q - 1, M2)
                if q + 1 < NQ:
                    diagonals(q + 1, NPART - 1)
                    if q:
                        copy_y(q - 1)
            q = NQ - 1
            copy_gram(q)
            act.wait_ge(z1_last_filled, 1)
            nc.scalar.activation(z_sb[:, 0, :], z1_out(q), ACT.Identity, bias=kbias[:, 0:1]).then_inc(z1_last_ready, 1)
            act.wait_ge(z_filled, NQ)
            nc.scalar.activation(z_sb[:, 1, :], z_bank[:, 0:P], ACT.Identity, bias=kbias[:, 1:2]).then_inc(z_ready, 1)
            for m in range(M1):
                act.wait_ge(h1_summed, NQ + m)
                nc.scalar.activation(h1_sb[:, m, :], h1_pre[:, m, :], ACT.Relu).then_inc(h1_ready, 1)
            copy_y(NQ - 2)
            act.wait_ge(h2_filled, NQ)
            relu_h2(NQ - 1, 1)
            copy_y(NQ - 1)

        @block.vector
        def _(dve):
            dve.wait_ge(cin_in, 32)
            eye = w1_sb[:].rearrange("p a b -> p (a b)")[:, 0:F * F:F + 1]
            for c, (f0, n) in enumerate(CLIQUES):
                for j in range(1, n):
                    o = LB + pair_col(c, j)
                    nc.vector.tensor_tensor(w1_pairs[:, o:o + j], w1_sb[:, f0:f0 + j, f0 + j],
                                            w1_sb[:, f0 + j, f0:f0 + j], ALU.add)
                o = LB + square_col(c)
                nc.vector.tensor_copy(w1_pairs[:, o:o + n], eye[:, f0:f0 + n])
            for o, u0, nu, v0, nv in ((XB, 0, A0, A0, C3), (SB, 0, C0, C0, C1 + C2), (RB, C0, C1, L2, C2)):
                nc.vector.tensor_tensor(
                    w1_pairs[:, o:o + nu * nv].rearrange("p (u v) -> p u v", v=nv),
                    w1_sb[:, u0:u0 + nu, v0:v0 + nv],
                    w1_sb[:, v0:v0 + nv, u0:u0 + nu].rearrange("p v u -> p u v"), ALU.add)
            nc.vector.tensor_copy(w1_pairs[:, UB:NCOL], cols_sb[:, 0:1]).then_inc(pairs_built, 1)
            nc.vector.tensor_scalar(kbias[:], b12, float(K), None, ALU.mult)
            nc.vector.memset(diag[:], 0.0)
            nc.vector.memset(gram[:, NX:P + GS], 0.0)
            nc.vector.memset(wgt2[:], 0.0)
            nc.vector.memset(sums2[SQ:UP], 0.0)
            nc.vector.memset(block2[:], 0.0).then_inc(cleared, 1)
            dve.wait_ge(cleared, 1)
            for g in range(NG):
                last = nc.vector.memset(diag[g * SQ:(g + 1) * SQ, :, F, g], 1.0)
            last.then_inc(cleared, 1)

            dve.wait_ge(hot_in, 16 * (2 + NF))
            nc.vector.tensor_copy(ids_f[:], ids_row[:]).then_inc(hot_steps, 1)
            dve.wait_ge(hot_steps, 1)
            nc.vector.tensor_scalar(from_first[:], ids_f[:], marks_sb[0:NA, 0:1], None,
                                    ALU.is_ge).then_inc(hot_steps, 1)
            dve.wait_ge(hot_steps, 2)
            nc.vector.scalar_tensor_tensor(hot[:], ids_f[:], marks_sb[0:NA, 1:2], from_first[:], ALU.is_le,
                                           ALU.mult).then_inc(hot_ready, 1)
            dve.wait_ge(ids_in, 16)
            nc.vector.tensor_copy(low_f[:], idx[:, :, OF:OF + NF].rearrange("p q f -> p f q")).then_inc(mask_steps, 1)
            dve.wait_ge(mask_steps, 1)
            big = float(3 << 22)
            nc.vector.tensor_scalar(quot[:], low_f[:], 1 / RP, (RP - 1) / (2 * RP), ALU.mult,
                                    ALU.subtract).then_inc(mask_steps, 1)
            dve.wait_ge(mask_steps, 2)
            nc.vector.tensor_scalar(quot_big[:], quot[:], big, None, ALU.add).then_inc(mask_steps, 1)
            dve.wait_ge(mask_steps, 3)
            nc.vector.tensor_scalar(quot_8[:], quot_big[:], big, float(RP), ALU.subtract,
                                    ALU.mult).then_inc(mask_steps, 1)
            dve.wait_ge(mask_steps, 4)
            nc.vector.tensor_tensor(low_id[:], low_f[:], quot_8[:], ALU.subtract).then_inc(mask_steps, 1)
            dve.wait_ge(mask_steps, 5)
            low, numbers = low_id[:].rearrange("p f q -> p (f q)"), marks_sb[:, 2:]
            nc.vector.tensor_tensor(
                mask[:].rearrange("p f q b -> p (f q) b"),
                bass.AP(numbers.tensor, numbers.offset, [list(numbers.ap[0]), [0, NF * NQ], [1, RP]]),
                bass.AP(low.tensor, low.offset, [list(low.ap[0]), [1, NF * NQ], [0, RP]]),
                ALU.is_equal).then_inc(mask_steps, 1)
            dve.wait_ge(pairs_built, 1)
            nc.vector.tensor_copy(block2[:, 0, 0:NX - P], w1_pairs[:, XB + P:UB])

            x = vmat[:, :, XB:UB].rearrange("p l (u a) -> p l u a", a=C3)
            s_ = vmat[:, :, SB:RB].rearrange("p l (u v) -> p l u v", v=C1 + C2)
            r = vmat[:, :, RB:LB]
            flat = vmat[:].rearrange("p l n -> p (l n)")

            def at(l, col, *dims):
                return bass.AP(flat.tensor, flat.offset + l * NCOL + col, [list(flat.ap[0]), *map(list, dims)])

            def add(dst, term):
                return nc.vector.tensor_tensor(dst, dst, term, ALU.add)

            def fold_squares():
                dve.wait_ge(v_out, F)
                nc.vector.tensor_copy(block2[:, 1, GS:GW], vmat[:, :, UB])
                nv = C1 + C2
                sq = [LB + square_col(c) for c in range(4)]
                for c, (f0, n) in enumerate(CLIQUES[:3]):
                    add(at(A0, sq[c], (NCOL, C3), (1, n)), at(f0, XB + f0 * C3, (1, C3), (NCOL + C3, n)))
                add(at(C0, sq[0], (NCOL, nv), (1, C0)), at(0, SB, (1, nv), (NCOL + nv, C0)))
                add(at(0, sq[1], (NCOL, C0), (1, C1)), at(C0, SB, (nv, C0), (NCOL + 1, C1)))
                add(at(L2, sq[1], (1, C1)), at(C0, RB, (NCOL + 1, C1)))
                add(at(0, sq[3], (NCOL, A0), (1, C3)), at(A0, XB, (C3, A0), (NCOL + 1, C3))).then_inc(v_folded, 1)

            def fold_v(second):
                dve.wait_ge(v_out, F)
                if second:
                    dve.wait_ge(v_folded, 2)
                for j in range(1, C0):
                    both = 2 if j < C1 else 1
                    dst = at(A0, LB + pair_col(0, j), (NCOL, C3), (START[1], both), (1, j))
                    if second:
                        add(dst, at(0, XB + j * C3, (1, C3), (C0 * (NCOL + C3), both), (NCOL, j)))
                    else:
                        add(dst, at(j, XB, (1, C3), (C0 * (NCOL + C3), both), (C3, j)))
                for j in range(1, C0):
                    o = LB + pair_col(0, j)
                    add(vmat[:, C0:A0, o:o + j], (s_[:, 0:j, j, :] if second else s_[:, j, 0:j, :])
                        .rearrange("p i v -> p v i"))
                for j in range(1, C1):
                    o = LB + pair_col(1, j)
                    add(vmat[:, 0:C0, o:o + j], s_[:, C0:C0 + j, :, j].rearrange("p i u -> p u i") if second
                        else s_[:, C0 + j, :, 0:j])
                    add(vmat[:, L2, o:o + j], r[:, C0:C0 + j, j] if second else r[:, C0 + j, 0:j])
                for j in range(1, C3):
                    o = LB + pair_col(3, j)
                    add(vmat[:, 0:A0, o:o + j], x[:, A0:A0 + j, :, j].rearrange("p i u -> p u i") if second
                        else x[:, A0 + j, :, 0:j])
                nv = C1 + C2
                dst = at(A0, SB, (NCOL, C3), (nv, C0), (1, nv))
                add(dst, at(0, XB + C0 * C3, (1, C3), (NCOL, C0), (C3, nv)) if second
                    else at(C0, XB, (1, C3), (C3, C0), (NCOL, nv)))
                add(vmat[:, A0:F, RB:LB], (x[:, C0:L2, L2, :] if second else x[:, L2, C0:L2, :])
                    .rearrange("p v a -> p a v"))
                last = add(s_[:, L2, :, 0:C1], r[:, 0:C0, :] if second
                           else s_[:, C0:L2, :, C1].rearrange("p v u -> p u v"))
                last.then_inc(v_folded, 1)

            def products(q, part, t0, t1):
                if q and part == 0:
                    dve.wait_ge(sum2_filled, q * T2)
                et = emb_t[:, q % 2]
                ts, steps = slice(t0, t1), t1 - t0

                def fields(a, n, clique=1):
                    return bass.AP(et.tensor, et.offset + a * SQ + t0,
                                   [list(et.ap[0]), [1, steps], [C0 * SQ, clique], [SQ, n]])

                def one_field(a, n, clique=1):
                    return bass.AP(et.tensor, et.offset + a * SQ + t0,
                                   [list(et.ap[0]), [1, steps], [C0 * SQ, clique], [0, n]])

                def place(o, n, clique=1):
                    p0 = prod[:, ts]
                    return bass.AP(p0.tensor, p0.offset + o, [list(p0.ap[0]), [NP, steps], [START[1], clique], [1, n]])

                for c, together, j0, j1 in (((0, 2, 1, C1), (0, 1, C1, C0)),
                                            *[((3, 1, max(f - A0, 1), f - A0 + n),) for f, n in PARTS[1:]])[part]:
                    f0 = CLIQUES[c][0]
                    for j in range(j0, j1):
                        last = nc.vector.tensor_tensor(place(pair_col(c, j), j, together), fields(f0, j, together),
                                                       one_field(f0 + j, j, together), ALU.mult)
                if part:
                    if part == NPART - 1:
                        last.then_inc(prod_ready, 1)
                    return
                o, nv = P, C1 + C2
                u_of = bass.AP(et.tensor, et.offset + t0, [list(et.ap[0]), [1, steps], [SQ, C0], [0, nv]])
                v_of = bass.AP(et.tensor, et.offset + C0 * SQ + t0,
                               [list(et.ap[0]), [1, steps], [0, C0], [SQ, nv]])
                nc.vector.tensor_tensor(prod[:, ts, o:o + C0 * nv].rearrange("p t (u v) -> p t u v", v=nv),
                                        u_of, v_of, ALU.mult)
                nc.vector.tensor_tensor(place(o + C0 * nv, C1), fields(C0, C1), one_field(L2, C1), ALU.mult)

            def fetch():
                dve.wait_ge(candidates_filled, 1)
                dve.wait_ge(mask_steps, 6)
                for f in range(NF):
                    for i in range(2):
                        m = mask[:, f, 2 * i:2 * i + 2]
                        kept = bass.AP(m.tensor, m.offset, [list(m.ap[0]), [1, 2 * RP], [0, K]])
                        last = nc.vector.tensor_tensor(
                            masked[:, f, 2 * i:2 * i + 2].rearrange("p q b k -> p (q b) k"),
                            candidates(f, i).rearrange("p q (b k) -> p (q b) k", k=K), kept, ALU.mult)
                last.then_inc(masked_ready, 1)
                dve.wait_ge(masked_ready, 1)
                for f in range(NF):
                    last = nc.vector.tensor_reduce(fetched[:, :, f], masked[:, f].rearrange("p q b k -> p q k b"),
                                                   AX.X, ALU.add)
                last.then_inc(fetch_done, 1)

            def place_fetched(q):
                dve.wait_ge(fetch_done, 1)
                if q >= 2:
                    dve.wait_ge(fields_summed, q - 1)
                nc.vector.tensor_copy(emb[:, q % 2, OF * K:(OF + NF) * K],
                                      fetched[:, q].rearrange("p f k -> p (f k)")).then_inc(placed, 1)

            def turn_and_multiply(q, part):
                f0, n = PARTS[part]
                dve.wait_ge(gathered[q][part], 16 * len(GATHERED[part]))
                if f0 <= OF < f0 + n:
                    dve.wait_ge(placed, q + 1)
                if q >= 2:
                    dve.wait_ge(diag_ready, ND_TILE * (q - 1))
                nc.vector.transpose(emb_t[:, q % 2, f0:f0 + n].rearrange("p f t -> p (f t)"),
                                    emb[:, q % 2, f0 * K:(f0 + n) * K]).then_inc(emb_turned, 1)
                dve.wait_ge(emb_turned, NPART * q + part + 1)
                for t0, t1 in STEPS[part]:
                    products(q, part, t0, t1)

            def cross_products(q):
                e = emb[:, q % 2]
                if q:
                    dve.wait_ge(gram_ready, q)
                for i in range(2):
                    u_of = bass.AP(e.tensor, e.offset + i * UH * K, [list(e.ap[0]), [K, UH], [0, C3], [1, K]])
                    a_of = bass.AP(e.tensor, e.offset + A0 * K, [list(e.ap[0]), [0, UH], [K, C3], [1, K]])
                    nc.vector.tensor_tensor(cross[:, i], u_of, a_of, ALU.mult).then_inc(crossed, 1)
                if q:
                    dve.wait_ge(gram_filled, q)
                nc.vector.tensor_reduce(gram[:, P + GS:], emb[:, q % 2].rearrange("p (f k) -> p f k", k=K),
                                        AX.X, ALU.add).then_inc(fields_summed, 1)

            def cross_sums(q):
                if q:
                    dve.wait_ge(gram_filled, q)
                for i in range(2):
                    dve.wait_ge(crossed, 2 * q + i + 1)
                    o = i * UH * C3
                    last = nc.vector.tensor_reduce(gram[:, o:o + UH * C3],
                                                   cross[:, i].rearrange("p u a k -> p (u a) k"), AX.X, ALU.add)
                last.then_inc(gram_ready, 1)

            def sum_h1(q):
                dve.wait_ge(h1_filled, q + 1)
                nc.vector.tensor_tensor(h1_pre[:], mlp_bank[:].rearrange("p (m c) -> p m c", m=M1),
                                        dense_h[:, :, q * P:(q + 1) * P], ALU.add).then_inc(h1_summed, 1)

            for q in range(NQ):
                turn_and_multiply(q, 0)
                if q == 0:
                    fetch()
                place_fetched(q)
                for part in range(1, NPART):
                    turn_and_multiply(q, part)
                if q == 0:
                    fold_squares()
                    fold_v(0)
                    fold_v(1)
                if q:
                    cross_sums(q - 1)
                cross_products(q)
                if q:
                    sum_h1(q - 1)
            cross_sums(NQ - 1)

            for m in range(M1):
                dve.wait_ge(h1_filled, NQ + m)
                nc.vector.tensor_tensor(h1_pre[:, m, :], h1_out(NQ - 1, m), dense_h[:, m, (NQ - 1) * P:],
                                        ALU.add).then_inc(h1_summed, 1)
            dve.wait_ge(h2_filled, NQ + 1)
            nc.vector.tensor_scalar(h2_sb[:, 1, :], h2_out(NQ - 1, 1), bt2[:, 1:2], 0.0, ALU.add,
                                    ALU.max).then_inc(h2_last_ready, 1)


def kernel(**inputs):
    import numpy as np
    import concourse.bacc as bacc
    from concourse.bass_utils import run_bass_kernel_spmd as run

    nc = bacc.Bacc("TRN2", target_bir_lowering=False, num_devices=1)
    arrays = {}

    def give(name, a):
        a = np.ascontiguousarray(a)
        arrays["in_" + name] = a
        return nc.dram_tensor("in_" + name, a.shape, mybir.dt.from_np(a.dtype), kind="ExternalInput").ap()

    ids = give("ids", inputs["ids"])
    ids_of = give("ids_of", np.asarray(inputs["ids"])[:, OF:OF + NF].T)
    marks = give("marks", np.concatenate([RP * np.arange(P)[:, None] + np.array([0, RP - 1]),
                                          np.broadcast_to(np.arange(RP), (P, RP))], axis=1).astype(np.float32))
    tables = [give(f"tbl_{f}", inputs[f"tbl_{f}"]) for f in range(F)]
    dense_t = give("dense_t", np.asarray(inputs["dense_ctx"]).reshape(NQ, NG, SQ, ND).transpose(3, 0, 2, 1)
                   .reshape(ND, NQ, P))
    w1 = give("w1", inputs["L0_rec_W1"])
    w2_t = give("w2_t", np.asarray(inputs["L0_rec_W2"]).transpose(1, 2, 0))
    vectors = [np.asarray(inputs[n]).reshape(-1, P) for n in ("L0_rec_b1", "L0_rec_b2", "b_top1", "b_top2", "W_top3")]
    columns = give("columns", np.concatenate(vectors).T)
    y = nc.dram_tensor("out_y", (B, 1), F32, kind="ExternalOutput").ap()
    build(nc, ids, ids_of, marks, tables, dense_t, w1, w2_t, columns, give("W_top1", inputs["W_top1"]),
          give("W_top2", inputs["W_top2"]), y)
    r = run(nc, [arrays], core_ids=[0])
    return r.results[0]["out_y"]
```
